# Optimizing a Trainium2 kernel written in Bass

```python
import numpy as np
import jax
import jax.numpy as jnp

def _softmax(x, axis=-1):
    return jax.nn.softmax(x, axis=axis)

def _gelu(x):
    return jax.nn.gelu(x, approximate=True)

def _silu(x):
    return jax.nn.silu(x)

def _sigmoid(x):
    return jax.nn.sigmoid(x)

def _layernorm(x, axis=-1, eps=1e-05):
    m = jnp.mean(x, axis=axis, keepdims=True)
    v = jnp.var(x, axis=axis, keepdims=True)
    return (x - m) / jnp.sqrt(v + eps)

def _scatter_add(tgt, idx, src, axis=0):
    return tgt.at[idx].add(src)

def _segment_sum(src, seg, n):
    return jax.ops.segment_sum(src, seg, n)
kernel_name = 'mk_gnn_resnorm_d2_gnn_r8_6b9563'

def setup_inputs(seed: int=0):
    np.random.seed(seed)
    _w = jnp.asarray

    def _rec_inputs():
        import jax
        import jax.numpy as jnp
        _gk = jax.random.key(seed)
        x = -0.0001006 + 1 * jax.random.normal(jax.random.fold_in(_gk, 1), (6250, 96), jnp.float32)
        _s = jax.random.randint(jax.random.fold_in(_gk, 2), (100000,), 0, 6250, jnp.int32)
        _d = jax.random.randint(jax.random.fold_in(_gk, 3), (100000,), 0, 6250, jnp.int32)
        _loop = jnp.arange(6250, dtype=jnp.int32)
        src = jnp.concatenate([_s, _d, _loop])
        dst = jnp.concatenate([_d, _s, _loop])
        _o = jnp.argsort(dst, stable=True)
        src = src[_o]
        dst = dst[_o]
        edge_attr_4 = 0.000714719 + 1.00021 * jax.random.normal(jax.random.fold_in(_gk, 11), (206250, 4), jnp.float32)
        return (x, src, dst, edge_attr_4)
    x, src, dst, edge_attr_4 = _rec_inputs()

    def _L0_gnn_setup():
        import jax, jax.numpy as jnp
        import numpy as np
        EPS = 1e-05

        def _mlp(h, W, b, gamma, beta):
            h = jax.nn.relu(h @ W + b)
            mu = jnp.mean(h, axis=0)
            var = jnp.mean(jnp.square(h - mu), axis=0)
            return gamma * (h - mu) * jax.lax.rsqrt(var + EPS) + beta
        key = jax.random.key(seed)
        ks = jax.random.split(key, 10)
        N, E, C_in, C_out, E_dim = (6250, 100000, 96, 96, 4)
        x = jax.random.normal(ks[0], (N, C_in), dtype=jnp.float32)
        edge_index = jax.random.randint(ks[1], (2, E), 0, N, dtype=jnp.int64)
        edge_attr = jax.random.normal(ks[2], (E, E_dim), dtype=jnp.float32)
        s = lambda fan_in: 1.0 / np.sqrt(fan_in)
        W_node = jax.random.uniform(ks[3], (C_in, C_out), jnp.float32, -s(C_in), s(C_in))
        b_node = jnp.zeros((C_out,), jnp.float32)
        g_node = jnp.ones((C_out,), jnp.float32)
        beta_node = jnp.zeros((C_out,), jnp.float32)
        W_edge = jax.random.uniform(ks[4], (E_dim, C_out), jnp.float32, -s(E_dim), s(E_dim))
        b_edge = jnp.zeros((C_out,), jnp.float32)
        g_edge = jnp.ones((C_out,), jnp.float32)
        beta_edge = jnp.zeros((C_out,), jnp.float32)
        M_in = 2 * C_in + C_out
        W_msg = jax.random.uniform(ks[5], (M_in, C_out), jnp.float32, -s(M_in), s(M_in))
        b_msg = jnp.zeros((C_out,), jnp.float32)
        g_msg = jnp.ones((C_out,), jnp.float32)
        beta_msg = jnp.zeros((C_out,), jnp.float32)
        return dict(x=x, edge_index=edge_index, edge_attr=edge_attr, W_node=W_node, b_node=b_node, g_node=g_node, beta_node=beta_node, W_edge=W_edge, b_edge=b_edge, g_edge=g_edge, beta_edge=beta_edge, W_msg=W_msg, b_msg=b_msg, g_msg=g_msg, beta_msg=beta_msg)
    _L0_gnn_all = _L0_gnn_setup()
    _L0_gnn_in = {k: v for k, v in _L0_gnn_all.items() if k in ('W_node', 'b_node', 'g_node', 'beta_node', 'W_edge', 'b_edge', 'g_edge', 'beta_edge', 'W_msg', 'b_msg', 'g_msg', 'beta_msg')}
    del _L0_gnn_all

    def _L1_gnn_setup():
        import jax, jax.numpy as jnp
        import numpy as np
        N_NODES = 6250
        N_EDGES = 100000
        DIM = 96
        HEADS = 4
        LAYERS = 3
        NEG_SLOPE = 0.2

        def _gat_layer(x, src, dst, W, a_src, a_dst, b):
            N = x.shape[0]
            H, C = a_src.shape
            h = (x @ W).reshape(N, H, C)
            alpha_s = jnp.einsum('nhc,hc->nh', h, a_src)
            alpha_d = jnp.einsum('nhc,hc->nh', h, a_dst)
            e = jax.nn.leaky_relu(alpha_s[src] + alpha_d[dst], NEG_SLOPE)
            m = jax.ops.segment_max(e, dst, num_segments=N)
            m = jnp.where(jnp.isfinite(m), m, 0.0)
            ex = jnp.exp(e - m[dst])
            den = jax.ops.segment_sum(ex, dst, num_segments=N)
            alpha = ex / (den[dst] + 1e-16)
            msg = h[src] * alpha[:, :, None]
            out = jax.ops.segment_sum(msg, dst, num_segments=N)
            return out.reshape(N, H * C) + b
        key = jax.random.key(seed)
        ks = jax.random.split(key, 6)
        C = DIM // HEADS
        x = jax.random.normal(ks[0], (N_NODES, DIM), dtype=jnp.float32)
        edge_index = jax.random.randint(ks[1], (2, N_EDGES), 0, N_NODES, dtype=jnp.int32)
        W = jax.random.normal(ks[2], (LAYERS, DIM, DIM), dtype=jnp.float32) * (1.0 / np.sqrt(DIM))
        att_src = jax.random.normal(ks[3], (LAYERS, HEADS, C), dtype=jnp.float32) * (1.0 / np.sqrt(C))
        att_dst = jax.random.normal(ks[4], (LAYERS, HEADS, C), dtype=jnp.float32) * (1.0 / np.sqrt(C))
        bias = jnp.zeros((LAYERS, DIM), dtype=jnp.float32)
        return {'x': x, 'edge_index': edge_index, 'W': W, 'att_src': att_src, 'att_dst': att_dst, 'bias': bias}
    _L1_gnn_all = _L1_gnn_setup()
    _L1_gnn_in = {k: v for k, v in _L1_gnn_all.items() if k in ('W', 'att_src', 'att_dst', 'bias')}
    del _L1_gnn_all
    return {'x': x, 'src': src, 'dst': dst, 'edge_attr_4': edge_attr_4, 'L0_gnn_W_node': _L0_gnn_in['W_node'], 'L0_gnn_b_node': _L0_gnn_in['b_node'], 'L0_gnn_g_node': _L0_gnn_in['g_node'], 'L0_gnn_beta_node': _L0_gnn_in['beta_node'], 'L0_gnn_W_edge': _L0_gnn_in['W_edge'], 'L0_gnn_b_edge': _L0_gnn_in['b_edge'], 'L0_gnn_g_edge': _L0_gnn_in['g_edge'], 'L0_gnn_beta_edge': _L0_gnn_in['beta_edge'], 'L0_gnn_W_msg': _L0_gnn_in['W_msg'], 'L0_gnn_b_msg': _L0_gnn_in['b_msg'], 'L0_gnn_g_msg': _L0_gnn_in['g_msg'], 'L0_gnn_beta_msg': _L0_gnn_in['beta_msg'], 'L1_gnn_W': _L1_gnn_in['W'], 'L1_gnn_att_src': _L1_gnn_in['att_src'], 'L1_gnn_att_dst': _L1_gnn_in['att_dst'], 'L1_gnn_bias': _L1_gnn_in['bias']}

def reference(x, src, dst, edge_attr_4, L0_gnn_W_node, L0_gnn_b_node, L0_gnn_g_node, L0_gnn_beta_node, L0_gnn_W_edge, L0_gnn_b_edge, L0_gnn_g_edge, L0_gnn_beta_edge, L0_gnn_W_msg, L0_gnn_b_msg, L0_gnn_g_msg, L0_gnn_beta_msg, L1_gnn_W, L1_gnn_att_src, L1_gnn_att_dst, L1_gnn_bias):
    import jax
    import jax.numpy as jnp

    def _L0_gnn_ref(x, edge_index, edge_attr, W_node, b_node, g_node, beta_node, W_edge, b_edge, g_edge, beta_edge, W_msg, b_msg, g_msg, beta_msg):
        import jax, jax.numpy as jnp
        import numpy as np
        EPS = 1e-05

        def _mlp(h, W, b, gamma, beta):
            h = jax.nn.relu(h @ W + b)
            mu = jnp.mean(h, axis=0)
            var = jnp.mean(jnp.square(h - mu), axis=0)
            return gamma * (h - mu) * jax.lax.rsqrt(var + EPS) + beta
        node_feat = _mlp(x, W_node, b_node, g_node, beta_node)
        edge_feat = _mlp(edge_attr, W_edge, b_edge, g_edge, beta_edge)
        row, col = (edge_index[0], edge_index[1])
        message = jnp.concatenate([x[row], x[col], edge_feat], axis=1)
        message = _mlp(message, W_msg, b_msg, g_msg, beta_msg)
        agg = jax.ops.segment_sum(message, col, num_segments=node_feat.shape[0])
        return agg + node_feat

    def _L1_gnn_ref(x, edge_index, W, att_src, att_dst, bias):
        import jax, jax.numpy as jnp
        import numpy as np
        N_NODES = 6250
        N_EDGES = 100000
        DIM = 96
        HEADS = 4
        LAYERS = 3
        NEG_SLOPE = 0.2

        def _gat_layer(x, src, dst, W, a_src, a_dst, b):
            N = x.shape[0]
            H, C = a_src.shape
            h = (x @ W).reshape(N, H, C)
            alpha_s = jnp.einsum('nhc,hc->nh', h, a_src)
            alpha_d = jnp.einsum('nhc,hc->nh', h, a_dst)
            e = jax.nn.leaky_relu(alpha_s[src] + alpha_d[dst], NEG_SLOPE)
            m = jax.ops.segment_max(e, dst, num_segments=N)
            m = jnp.where(jnp.isfinite(m), m, 0.0)
            ex = jnp.exp(e - m[dst])
            den = jax.ops.segment_sum(ex, dst, num_segments=N)
            alpha = ex / (den[dst] + 1e-16)
            msg = h[src] * alpha[:, :, None]
            out = jax.ops.segment_sum(msg, dst, num_segments=N)
            return out.reshape(N, H * C) + b
        src = edge_index[0]
        dst = edge_index[1]
        for l in range(W.shape[0]):
            x = jax.nn.relu(_gat_layer(x, src, dst, W[l], att_src[l], att_dst[l], bias[l]))
        return x
    edge_index = jnp.stack([src, dst])
    x = _layernorm(x + _L0_gnn_ref(x, edge_index, edge_attr_4, L0_gnn_W_node, L0_gnn_b_node, L0_gnn_g_node, L0_gnn_beta_node, L0_gnn_W_edge, L0_gnn_b_edge, L0_gnn_g_edge, L0_gnn_beta_edge, L0_gnn_W_msg, L0_gnn_b_msg, L0_gnn_g_msg, L0_gnn_beta_msg), axis=-1)
    x = _layernorm(x + _L1_gnn_ref(x, edge_index, L1_gnn_W, L1_gnn_att_src, L1_gnn_att_dst, L1_gnn_bias), axis=-1)
    return x

_drawn_inputs = setup_inputs


def setup_inputs(seed=0):
    import zlib

    import numpy as np

    out = dict(_drawn_inputs(seed))
    spreads = {'L0_gnn_b_node': (0.0, 0.8),
     'L0_gnn_g_node': (1.0, 0.6),
     'L0_gnn_beta_node': (0.0, 0.8),
     'L0_gnn_b_edge': (0.0, 0.1),
     'L0_gnn_g_edge': (1.0, 0.2),
     'L0_gnn_beta_edge': (0.0, 0.389),
     'L0_gnn_b_msg': (0.0, 0.1),
     'L0_gnn_g_msg': (1.0, 0.2),
     'L0_gnn_beta_msg': (0.0, 0.1),
     'L1_gnn_bias': (0.0, 0.1)}
    factors = {'L1_gnn_att_dst': 8.0}
    for name, (base, spread) in spreads.items():
        noise = np.random.default_rng([zlib.crc32(name.encode()), seed]).standard_normal(out[name].shape)
        drawn = base * np.exp(spread * noise) if base else spread * noise
        out[name] = jnp.asarray(drawn.astype(out[name].dtype))
    for name, factor in factors.items():
        out[name] = (out[name] * factor).astype(out[name].dtype)
    return out
```

```python
from contextlib import ExitStack

import concourse.bass as bass
from concourse import mybir

ALU = mybir.AluOpType
ACT = mybir.ActivationFunctionType
AX = mybir.AxisListType
F32 = mybir.dt.float32
I32 = mybir.dt.int32

P = 128
N, E, D, DE = 6250, 206250, 96, 4
LAYERS, H = 3, 4
C = D // H
EPS = 1e-5
SLOPE = 0.2
GAIN = 1 / SLOPE - 1

TPG = 8
GE = P * TPG
NG = -(-E // GE)
EPAD = NG * GE
NT = -(-N // P)
NPAD = NT * P
RING = 8
ERING = 4
LAG = 3

WA = 32
NWA = NPAD // WA
WM = P
NWM = NPAD // WM
ROWS_A = -(-(NG * NWA + 1) // P) * P
ROWS_M = -(-(NG * NWM + 1) // P) * P

TW = D + 1 + H
ZW = WA - 1 + P
MW = 2 * D + 1
CH = 512
FULL = E // CH
SPAN = 8
SURE = 4
KG = -(-NG // P)

MASKED = -1e30
FLOOR = 1e20


def gnn_kernel(nc, x, xT, src, dst, edgeT, Wn, bn, gn, betan, We, be, ge, betae,
               Wm, bm, gm, betam, Wl, WlT, att_src, att_dst, bias, out):
    with ExitStack() as ctx:
        def sb(name, shape, dt=F32):
            return ctx.enter_context(nc.sbuf_tensor(name, shape, dt))

        def dram(name, shape, dt=F32):
            return nc.dram_tensor(name, shape, dt).ap()

        names = []

        def sem(name):
            names.append(name)
            return ctx.enter_context(nc.semaphore(name))

        table_m = dram("table_m", (NPAD, D))
        table_a = dram("table_a", (NPAD, TW))
        steps_a = dram("steps_a", (ROWS_A, 4), I32)
        steps_m = dram("steps_m", (ROWS_M, 4), I32)

        iota = sb("iota", [P, 2 * P])
        part = sb("part", [P, 1])
        part_i = sb("part_i", [P, 4], I32)
        ident = sb("ident", [P, P])
        fold = sb("fold", [P, WA])
        headmask = sb("headmask", [P, D])
        rowmask = sb("rowmask", [P, 1])
        ones = sb("ones", [P, P])
        base_a = sb("base_a", [P, NWA + 1])
        base_m = sb("base_m", [P, NWM + 1])
        dstf = sb("dstf", [P, NG * TPG])
        ctl = sb("ctl", [1, 8], I32)
        ends_a = sb("ends_a", [1, NG], I32)
        ends_m = sb("ends_m", [1, NG], I32)
        idx = sb("idx", [P, RING, TPG], I32)
        rows = sb("rows", [P, RING, TPG, TW])
        XT = sb("XT", [D + 1, NPAD])
        xn = sb("xn", [P, NT, D])
        big = sb("big", [P, NWA + 1, D + 1])
        w_all = sb("w_all", [D + 1, LAYERS, TW])
        z_all = sb("z_all", [D, LAYERS, ZW])
        bias_all = sb("bias_all", [D, LAYERS])
        w_l = sb("w_l", [D + 1, TW])
        z_l = sb("z_l", [D, ZW])
        bias_l = sb("bias_l", [D, 1])
        small = sb("small", [P, 64])
        rowsb = sb("rowsb", [P, 8, D])
        work = sb("work", [P, 9472])
        lnst = sb("lnst", [P, NT, 6])
        lnmv = sb("lnmv", [P, NT, 2])
        lnr = sb("lnr", [P, NT])

        ps = ctx.enter_context(nc.psum_tensor("ps", [P, 8, 512], F32))

        def bank(b, rows_, cols):
            return ps[0:rows_, b, 0:cols]

        s_load = sem("s_load")
        s_iota = sem("s_iota")
        s_const = sem("s_const")
        s_v = sem("s_v")
        s_a = sem("s_a")
        s_p = sem("s_p")
        s_q = sem("s_q")

        wt = dict(
            Wn=sb("sWn", [D, D]), W1=sb("sW1", [D, D]), W2=sb("sW2", [D, D]), W3=sb("sW3", [D, D]),
            We=sb("sWe", [DE, D]), cols=sb("cols", [D, 8]),
            WT=sb("sWT", [D, LAYERS, D]), att=sb("att", [D, LAYERS, 2 * H]),
        )
        cols = wt["cols"]
        W3s = sb("W3s", [D, D])
        LOADS = 13 + 2 * H

        def column(v):
            return v.rearrange("(c o) -> c o", o=1)

        def row(v):
            return v.rearrange("(o c) -> o c", o=1)

        with nc.Block() as block:
            @block.sync
            def _(sp):
                dsti = work[:, 0:NG * TPG].bitcast(I32)
                with nc.allow_non_contiguous_dma(reason="columns of channels"):
                    sp.dma_start(dsti.rearrange("p (g j) -> p g j", j=TPG),
                                 dst.rearrange("(g p j) -> p g j", p=P, j=TPG)).then_inc(s_load, 16)
                    sp.dma_start(XT[0:D, :], xT).then_inc(s_load, 16)
                    sp.dma_start(xn[:, 0:NT - 1, :], x[0:(NT - 1) * P, :].rearrange("(t p) c -> p t c", p=P)).then_inc(s_load, 16)
                    sp.dma_start(wt["Wn"][:], Wn).then_inc(s_load, 16)
                    for k in range(3):
                        sp.dma_start(wt[f"W{k + 1}"][:], Wm[k * D:(k + 1) * D, :]).then_inc(s_load, 16)
                    sp.dma_start(wt["We"][:], We).then_inc(s_load, 16)
                    sp.dma_start(wt["WT"][:], WlT.rearrange("l o i -> o l i")).then_inc(s_load, 16)
                    sp.dma_start(bias_all[:], bias.rearrange("l c -> c l")).then_inc(s_load, 16)
                    sp.dma_start(rowsb[0:1, 0, :], row(bm)).then_inc(s_load, 16)
                    for k, v in enumerate((bn, gn, betan, be, ge, betae)):
                        sp.dma_start(cols[:, k:k + 1], column(v)).then_inc(s_load, 16)
                    for k, v in enumerate((gm, betam)):
                        sp.dma_start(rowsb[0:1, 1 + k, :], row(v)).then_inc(s_load, 16)
                    sp.wait_ge(s_const, 1)
                    sp.dma_start(w_all[0:D, :, 0:D], Wl.rearrange("l i o -> i l o")).then_inc(s_load, 16)
                    sp.dma_start(xn[0:N - (NT - 1) * P, NT - 1, :], x[(NT - 1) * P:N, :]).then_inc(s_load, 16)
                    for h in range(H):
                        for k, v in enumerate((att_src, att_dst)):
                            sp.dma_start(wt["att"][h * C:(h + 1) * C, :, k * H + h:k * H + h + 1],
                                         v[:, h, :].rearrange("l (c o) -> c l o", o=1)).then_inc(s_load, 16)
            LOADED = 16 * (12 + 6 + 2 + 1 + 2 * H)

            @block.gpsimd
            def _(pool):
                pool.iota(iota[:], [[1, 2 * P]], base=0, channel_multiplier=0,
                          allow_small_or_imprecise_dtypes=True).then_inc(s_iota, 1)
                pool.iota(part[:], [[0, 1]], base=0, channel_multiplier=1,
                          allow_small_or_imprecise_dtypes=True).then_inc(s_iota, 1)
                pool.iota(part_i[:, 0:1], [[0, 1]], base=0, channel_multiplier=1).then_inc(s_iota, 1)
                pool.iota(base_a[:], [[WA, NWA + 1]], base=0, channel_multiplier=0,
                          allow_small_or_imprecise_dtypes=True).then_inc(s_iota, 1)
                pool.iota(base_m[:], [[WM, NWM + 1]], base=0, channel_multiplier=0,
                          allow_small_or_imprecise_dtypes=True).then_inc(s_iota, 1)
                pool.iota(headmask[:].rearrange("p (h c) -> p h c", c=C), [[1, H], [0, C]], base=0,
                          channel_multiplier=0, allow_small_or_imprecise_dtypes=True).then_inc(s_iota, 1)

            @block.vector
            def _(dve):
                dve.memset(wt["att"][:], 0.0)
                dve.memset(xn[:, NT - 1, :], 0.0)
                dve.memset(XT[D:D + 1, :], 1.0)
                dve.memset(w_all[:], 0.0)
                dve.memset(z_all[:], 0.0)
                dve.memset(ones[:], 1.0).then_inc(s_const, 1)
                dve.wait_ge(s_const, 1)
                dve.memset(w_all[D:D + 1, :, D:D + 1], 1.0)
                dve.wait_ge(s_iota, 6)
                dve.tensor_scalar(ident[:], iota[:, 0:P], part[:, 0:1], None, ALU.is_equal)
                dve.tensor_scalar(part_i[:, 1:2], part_i[:, 0:1], 5, None, ALU.arith_shift_right)
                dve.tensor_scalar(part_i[:, 2:3], part_i[:, 0:1], WA - 1, None, ALU.bitwise_and)
                dve.tensor_scalar(rowmask[:], part[:], float(N - (NT - 1) * P), None, ALU.is_lt).then_inc(s_const, 1)
                dve.wait_ge(s_const, 2)
                dve.tensor_copy(small[:, 0:2], part_i[:, 1:3]).then_inc(s_const, 1)
                dve.wait_ge(s_const, 3)
                dve.tensor_scalar(fold[:], iota[:, 0:WA], small[:, 1:2], None, ALU.is_equal)
                dve.tensor_scalar(headmask[:], headmask[:], small[:, 0:1], None, ALU.is_equal).then_inc(s_const, 1)
                dve.wait_ge(s_load, LOADED)
                dve.tensor_copy(dstf[:], work[:, 0:NG * TPG].bitcast(I32)).then_inc(s_const, 1)
                dve.wait_ge(s_const, 5)

        def build_steps(tag, shift, nw, steps, ends, pairs_at):
            lo_hi = small[:, 8:8 + 2 * KG]
            lo_hi_i = sb(f"lohi_{tag}", [P, 2 * KG], I32)
            gmm = work[:, 2048:2048 + 2 * NG].rearrange("p (k g) -> p k g", k=2)
            tri = work[:, 2560:2560 + KG * NG].rearrange("p (k g) -> p k g", k=KG)
            eye = work[:, 3072:3072 + KG * NG].rearrange("p (k g) -> p k g", k=KG)
            spread = work[:, 3584:3584 + KG * 2 * P].rearrange("p (k v m) -> p k v m", k=KG, v=2)
            endv = work[:, 4608:4608 + 2 * NG].rearrange("p (v g) -> p v g", v=2)
            hit = work[:, 5120:5120 + NG]
            rec = sb(f"rec_{tag}", [P, 4], I32)
            s_red, s_tr, s_mm, s_ends, s_rec, s_sent, s_d, s_l = (
                sem(f"{n}_{tag}") for n in ("s_red", "s_tr", "s_mm", "s_ends", "s_rec", "s_sent", "s_d", "s_l"))
            sizes = [min(P, NG - k * P) for k in range(KG)]
            with nc.Block() as block:
                @block.vector
                def _(dve):
                    n = 0

                    def link(ins):
                        nonlocal n
                        n += 1
                        ins.then_inc(s_d, 1)
                        dve.wait_ge(s_d, n)

                    view = dstf[:].rearrange("p (g j) -> p g j", j=TPG)
                    dve.tensor_reduce(gmm[:, 0, :], view, AX.X, ALU.min)
                    dve.tensor_reduce(gmm[:, 1, :], view, AX.X, ALU.max).then_inc(s_red, 1)
                    link(dve.memset(lo_hi, 0.0))
                    for k in range(KG):
                        link(dve.tensor_scalar(small[:, 20:21], part[:], float(k * P), None, ALU.add))
                        dve.tensor_scalar(tri[:, k, :], iota[:, 0:NG], small[:, 20:21], None, ALU.is_ge)
                        link(dve.tensor_scalar(eye[:, k, :], iota[:, 0:NG], small[:, 20:21], None, ALU.is_equal))
                    dve.wait_ge(s_tr, 1)
                    for k in range(KG):
                        m = sizes[k]
                        dve.tensor_reduce(lo_hi[0:m, k:k + 1], ps[0:m, k, 0:P], AX.X, ALU.min)
                        link(dve.tensor_reduce(lo_hi[0:m, KG + k:KG + k + 1], ps[0:m, k, P:2 * P], AX.X, ALU.max))
                    link(dve.tensor_copy(lo_hi_i[:], lo_hi))
                    link(dve.tensor_scalar(lo_hi_i[:], lo_hi_i[:], shift, None, ALU.arith_shift_right))
                    link(dve.tensor_copy(lo_hi, lo_hi_i[:]))
                    link(dve.tensor_scalar(lo_hi[:, KG:], lo_hi[:, KG:], 1.0, None, ALU.add))
                    link(dve.tensor_tensor(lo_hi[:, 0:KG], lo_hi[:, KG:], lo_hi[:, 0:KG], ALU.subtract))
                    for k in range(KG):
                        dve.tensor_scalar(spread[:, k, 0, :], ones[:], lo_hi[:, k:k + 1], None, ALU.mult)
                        last = dve.tensor_scalar(spread[:, k, 1, :], ones[:], lo_hi[:, KG + k:KG + k + 1], None, ALU.mult)
                    last.then_inc(s_red, 1)
                    dve.wait_ge(s_mm, 1)
                    link(dve.tensor_copy(endv[:, 0, :], ps[:, 2, 0:NG]))
                    link(dve.tensor_tensor(endv[:, 1, :], ps[:, 3, 0:NG], endv[:, 0, :], ALU.subtract))
                    dve.tensor_copy(ends[:], endv[0:1, 0, :]).then_inc(s_ends, 1)
                    dve.wait_ge(s_ends, 1)
                    dve.tensor_scalar(ctl[0:1, 6:7], ends[0:1, NG - 1:NG], 7, None, ALU.arith_shift_right).then_inc(s_ends, 1)
                    dve.tensor_copy(small[0:1, 24:25], ends[0:1, NG - 1:NG]).then_inc(s_ends, 1)
                    dve.wait_ge(s_ends, 3)
                    link(dve.tensor_scalar(small[0:1, 24:25], small[0:1, 24:25], 1.0 - 2 * SURE, None, ALU.add))
                    link(dve.tensor_copy(small[0:1, 26:27], ctl[0:1, 6:7]))
                    link(dve.tensor_scalar(small[0:1, 26:27], small[0:1, 26:27], 1.0, None, ALU.add))
                    link(dve.tensor_copy(ctl[0:1, 6:7], small[0:1, 24:25]))
                    dve.tensor_copy(ctl[0:1, pairs_at + 1:pairs_at + 2], small[0:1, 26:27])
                    link(dve.tensor_scalar(ctl[0:1, pairs_at:pairs_at + 1], ctl[0:1, 6:7], 1, None, ALU.arith_shift_right))
                    link(dve.tensor_copy(small[:, 28:29], part[:]))

                @block.tensor
                def _(pe):
                    pe.wait_ge(s_red, 1)
                    for k in range(KG):
                        for v in range(2):
                            last = pe.transpose(ps[0:sizes[k], k, v * P:(v + 1) * P],
                                                gmm[:, v, k * P:k * P + sizes[k]], ident[:])
                    last.then_inc(s_tr, 1)
                    pe.wait_ge(s_red, 2)
                    for k in range(KG):
                        m = sizes[k]
                        pe.matmul(bank(2, P, NG), spread[0:m, k, 0, :], tri[0:m, k, :], start=(k == 0), stop=(k == KG - 1))
                    for k in range(KG):
                        m = sizes[k]
                        last = pe.matmul(bank(3, P, NG), spread[0:m, k, 1, :], eye[0:m, k, :], start=(k == 0), stop=(k == KG - 1))
                    last.then_inc(s_mm, 1)

            with nc.Block() as block:
                most = ROWS_A // P if nw == NWA else ROWS_M // P

                @block.vector
                def _(dve):
                    chunks = dve.value_load(ctl[0:1, pairs_at + 1:pairs_at + 2], min_val=1, max_val=most)
                    with dve.Fori(0, chunks) as c:
                        q, gcount, gsel, wsel = (small[:, k:k + 1] for k in (28, 29, 30, 31))
                        dve.tensor_scalar(hit, endv[:, 0, :], q, 0.0, ALU.is_le, ALU.add, accum_out=gcount).then_inc(s_l, 1)
                        dve.wait_ge(s_l, 7 * c + 1)
                        dve.tensor_scalar(hit, iota[:, 0:NG], gcount, None, ALU.is_equal).then_inc(s_l, 1)
                        dve.wait_ge(s_l, 7 * c + 2)
                        dve.tensor_tensor_reduce(out=hit, in0=hit, in1=endv[:, 1, :], scale=1.0, scalar=0.0,
                                                 op0=ALU.mult, op1=ALU.add, accum_out=wsel).then_inc(s_l, 1)
                        dve.tensor_scalar(gsel, gcount, float(NG - 1), None, ALU.min).then_inc(s_l, 1)
                        dve.wait_ge(s_l, 7 * c + 4)
                        dve.scalar_tensor_tensor(wsel, wsel, 0.0, q, ALU.add, ALU.add).then_inc(s_l, 1)
                        dve.wait_ge(s_l, 7 * c + 5)
                        dve.tensor_scalar(rec[:, 0:1], wsel, float(nw), None, ALU.min)
                        dve.tensor_copy(rec[:, 1:2], gsel).then_inc(s_l, 1)
                        dve.wait_ge(s_l, 7 * c + 6)
                        dve.tensor_scalar(rec[:, 2:3], rec[:, 1:2], RING - 1, None, ALU.bitwise_and)
                        dve.tensor_scalar(rec[:, 3:4], rec[:, 1:2], ERING - 1, None, ALU.bitwise_and).then_inc(s_rec, 1)
                        dve.tensor_scalar(q, q, float(P), None, ALU.add).then_inc(s_l, 1)
                        dve.wait_ge(s_l, 7 * c + 7)
                        dve.wait_ge(s_sent, 16 * c + 16)

                @block.sync
                def _(sp):
                    chunks = sp.value_load(ctl[0:1, pairs_at + 1:pairs_at + 2], min_val=1, max_val=most)
                    with sp.Fori(0, chunks) as c:
                        sp.wait_ge(s_rec, c + 1)
                        sp.dma_start(steps[bass.ds(c * P, P), :], rec[:]).then_inc(s_sent, 16)
                    sp.wait_ge(s_sent, 16)

        build_steps("m", 7, NWM, steps_m, ends_m, 0)
        build_steps("a", 5, NWA, steps_a, ends_a, 2)

        TAIL = E - FULL * CH
        MACRO = FULL // SPAN
        REST = FULL - MACRO * SPAN
        e_in = work[0:DE, 0:2 * SPAN * CH].rearrange("p (b n) -> p b n", b=2)
        relu_u = rows[0:D, :, :, :].rearrange("p r j c -> p (r j c)")[:, 0:4 * CH].rearrange("p (b n) -> p b n", b=4)
        estat = big[0:D, :, :].rearrange("p w c -> p (w c)")[:, 0:(FULL + 1) * 6].rearrange("p (n s) -> p n s", s=6)
        s_ein = [sem(f"s_ein{b}") for b in range(2)]
        s_u = sem("s_u")
        s_ru = sem("s_ru")
        s_st = sem("s_st")
        s_ew = sem("s_ew")
        s_sq = sem("s_sq")
        with nc.Block() as block:
            @block.sync
            def _(sp):
                for b in range(2):
                    sp.dma_start(e_in[:, b, :], edgeT[:, b * SPAN * CH:(b + 1) * SPAN * CH]).then_inc(s_ein[b], 16)
                with sp.Fori(1, MACRO // 2) as i:
                    for b in range(2):
                        sp.wait_ge(s_u, 2 * SPAN * i - SPAN + SPAN * b)
                        sp.dma_start(e_in[:, b, :],
                                     edgeT[:, bass.ds(i * (2 * SPAN * CH) + b * SPAN * CH, SPAN * CH)]).then_inc(s_ein[b], 16)
                sp.wait_ge(s_u, MACRO * SPAN)
                rest = E - MACRO * SPAN * CH
                sp.dma_start(e_in[:, 0, 0:rest], edgeT[:, MACRO * SPAN * CH:E]).then_inc(s_ein[0], 16)

            @block.tensor
            def _(pe):
                def chunk(b, j, k, n=CH):
                    pe.matmul(bank(k % 4, D, n), wt["We"][:], e_in[:, b, j * CH:j * CH + n],
                              start=True, stop=True).then_inc(s_u, 1)
                for b in range(2):
                    pe.wait_ge(s_ein[b], 16)
                    for j in range(SPAN):
                        k = b * SPAN + j
                        if k >= 4:
                            pe.wait_ge(s_ru, k - 3)
                        chunk(b, j, k)
                with pe.Fori(1, MACRO // 2) as i:
                    for b in range(2):
                        pe.wait_ge(s_ein[b], 16 * i + 16)
                        for j in range(SPAN):
                            pe.wait_ge(s_ru, 2 * SPAN * i + (b * SPAN + j - 3))
                            chunk(b, j, j)
                pe.wait_ge(s_ein[0], 16 * (MACRO // 2) + 16)
                for j in range(REST + 1):
                    k = MACRO * SPAN + j
                    pe.wait_ge(s_ru, k - 3)
                    chunk(0, j, k, CH if j < REST else TAIL)

            @block.scalar
            def _(act):
                def chunk(k, n=CH):
                    nc.scalar.activation(relu_u[:, k % 4, 0:n], bank(k % 4, D, n), ACT.Relu,
                                         bias=cols[:, 3:4]).then_inc(s_ru, 1)
                act.preload_act_table(ACT.Exp)
                for k in range(8):
                    act.wait_ge(s_u, k + 1)
                    if k >= 4:
                        act.wait_ge(s_st, k - 3)
                    chunk(k)
                with act.Fori(1, FULL // 8) as i:
                    for j in range(8):
                        act.wait_ge(s_u, 8 * i + j + 1)
                        act.wait_ge(s_st, 8 * i + (j - 3))
                        chunk(j)
                for k in range(FULL // 8 * 8, FULL + 1):
                    act.wait_ge(s_u, k + 1)
                    act.wait_ge(s_st, k - 3)
                    chunk(k, CH if k < FULL else TAIL)
                act.wait_ge(s_ew, 3)
                nc.scalar.activation(small[0:D, 32:34], small[0:D, 34:36], ACT.Sqrt).then_inc(s_sq, 1)

            @block.vector
            def _(dve):
                with dve.Fori(0, FULL // 4) as i:
                    for j in range(4):
                        dve.wait_ge(s_ru, 4 * i + j + 1)
                        dve.bn_stats(estat[:, bass.ds(4 * i + j, 1), :].rearrange("p n s -> p (n s)"), relu_u[:, j, :]).then_inc(s_st, 1)
                for k in range(FULL // 4 * 4, FULL + 1):
                    dve.wait_ge(s_ru, k + 1)
                    n = CH if k < FULL else TAIL
                    dve.bn_stats(estat[:, k, :], relu_u[:, k % 4, 0:n]).then_inc(s_st, 1)
                dve.wait_ge(s_st, FULL + 1)
                dve.bn_aggr(small[0:D, 36:38], estat.rearrange("p n s -> p (n s)")).then_inc(s_ew, 1)
                dve.wait_ge(s_ew, 1)
                dve.tensor_scalar(small[0:D, 34:36], small[0:D, 36:38], EPS, None, ALU.add).then_inc(s_ew, 2)
                dve.wait_ge(s_sq, 1)
                dve.reciprocal(small[0:D, 38:39], small[0:D, 33:34]).then_inc(s_ew, 1)
                dve.wait_ge(s_ew, 4)
                dve.tensor_tensor(small[0:D, 39:40], small[0:D, 38:39], cols[:, 4:5], ALU.mult).then_inc(s_ew, 1)
                dve.wait_ge(s_ew, 5)
                dve.tensor_scalar(W3s[:], wt["W3"][:], small[0:D, 39:40], None, ALU.mult)
                dve.tensor_tensor(small[0:D, 40:41], small[0:D, 36:37], small[0:D, 39:40], ALU.mult).then_inc(s_ew, 1)
                dve.wait_ge(s_ew, 6)
                dve.tensor_tensor(small[0:D, 41:42], cols[:, 5:6], small[0:D, 40:41], ALU.subtract).then_inc(s_ew, 1)

        nfT = XT[0:D, :]
        flat = big[:].rearrange("p w c -> p (w c)")
        B_AT, RING_AT = (NWM + 1) * MW, (NWM + 1) * (MW + D)
        acc_m = flat[:, 0:B_AT].rearrange("p (w c) -> p w c", c=MW)
        b_rows = flat[:, B_AT:RING_AT].rearrange("p (t c) -> p t c", c=D)
        edge_ring = flat[0:DE, RING_AT:RING_AT + ERING * GE].rearrange("p (r n) -> p r n", r=ERING)
        stage_m = work[:, 0:NT * D].rearrange("p (t c) -> p t c", c=D)
        s_c1 = sem("s_c1")
        s_c2 = sem("s_c2")
        s_t1 = sem("s_t1")
        s_t2 = sem("s_t2")
        s_tab = sem("s_tab")
        s_w = sem("s_w")
        s_wc = sem("s_wc")
        s_n = sem("s_n")
        s_nf = sem("s_nf")
        TB = 4
        NB = -(-NT // TB)
        tiles = [list(range(b * TB, min(NT, b * TB + TB))) for b in range(NB)]
        with nc.Block() as block:
            @block.tensor
            def _(pe):
                pe.matmul(ps[0:1, 7, 0:D], small[0:D, 41:42], wt["W3"][:], start=True, stop=True).then_inc(s_c1, 1)
                for l in range(LAYERS):
                    last = pe.matmul(ps[0:D, 6, l * 2 * H:(l + 1) * 2 * H], wt["WT"][:, l, :], wt["att"][:, l, :],
                                     start=True, stop=True)
                last.then_inc(s_w, 1)
                for b, ts in enumerate(tiles):
                    if b >= 2:
                        pe.wait_ge(s_t2, b - 1)
                    for t in ts:
                        last = pe.matmul(ps[:, b % 2, (t - ts[0]) * D:(t - ts[0] + 1) * D], XT[0:D, t * P:(t + 1) * P],
                                         wt["W1"][:], start=True, stop=True)
                    last.then_inc(s_t1, 1)
                pe.wait_ge(s_c2, 1)
                for b, ts in enumerate(tiles):
                    pe.wait_ge(s_t2, NB + b - 1)
                    for t in ts:
                        o = ps[:, (NB + b) % 2, (t - ts[0]) * D:(t - ts[0] + 1) * D]
                        pe.matmul(o, XT[0:D, t * P:(t + 1) * P], wt["W2"][:], start=True, stop=False)
                        last = pe.matmul(o, ones[0:1, :], rowsb[0:1, 3, :], start=False, stop=True)
                    last.then_inc(s_t1, 1)
                for b in range(NB):
                    n = min(512, NPAD - b * 512)
                    if b >= 4:
                        pe.wait_ge(s_nf, b - 3)
                    pe.matmul(bank(2 + b % 4, D, n), wt["Wn"][:], XT[0:D, b * 512:b * 512 + n],
                              start=True, stop=True).then_inc(s_n, 1)

            @block.vector
            def _(dve):
                dve.wait_ge(s_c1, 1)
                dve.tensor_tensor(rowsb[0:1, 3, :], ps[0:1, 7, 0:D], rowsb[0:1, 0, :], ALU.add).then_inc(s_c2, 1)
                dve.wait_ge(s_w, 1)
                got = ps[0:D, 6, 0:LAYERS * 2 * H].rearrange("p (l k h) -> p l k h", l=LAYERS, k=2)
                dve.tensor_copy(w_all[0:D, :, D + 1:TW], got[:, :, 0, :])
                dve.tensor_copy(z_all[:, :, WA - 1:ZW:WA], got[:, :, 1, :])
                dve.memset(b_rows[:, NT, :], 0.0)
                for k in range(2):
                    for b, ts in enumerate(tiles):
                        dve.wait_ge(s_t1, k * NB + b + 1)
                        to = stage_m if k == 0 else b_rows
                        dve.tensor_copy(to[:, ts[0]:ts[-1] + 1, :],
                                        ps[:, (k * NB + b) % 2, 0:len(ts) * D].rearrange("p (t c) -> p t c", c=D)).then_inc(s_t2, 1)
                dve.memset(acc_m, 0.0)

            @block.sync
            def _(sp):
                sp.wait_ge(s_t2, NB)
                sp.dma_start(table_m.rearrange("(t p) c -> p t c", p=P), stage_m).then_inc(s_tab, 16)
                sp.wait_ge(s_tab, 16)

            @block.scalar
            def _(act):
                for b in range(NB):
                    n = min(512, NPAD - b * 512)
                    act.wait_ge(s_n, b + 1)
                    nc.scalar.activation(nfT[:, b * 512:b * 512 + n], bank(2 + b % 4, D, n), ACT.Relu,
                                         bias=cols[:, 0:1]).then_inc(s_nf, 1)

        def edge_block(steps, ends, pairs_at, max_pairs, nw, table, width, with_edges, emit, passes):
            s_idx = [emit.sems[f"idx{k}"] for k in range(RING)]
            s_gat = [emit.sems[f"gat{k}"] for k in range(RING)]
            s_edge = [emit.sems[f"edge{k}"] for k in range(RING)]
            landed, begun, done = emit.sems["landed"], emit.sems["begun"], emit.sems["done"]
            src_v = src.rearrange("(g p j) -> g p j", p=P, j=TPG)

            with nc.Block() as block:
                @block.sync
                def _(sp):
                    def load_indices(g, k):
                        sp.dma_start(idx[:, k, :], src_v[g] if isinstance(g, int) else
                                     src_v[bass.ds(g, 1)].rearrange("g p j -> p (g j)")).then_inc(s_idx[k], 16)

                    def load_edges(g, k):
                        sp.dma_start(edge_ring[:, k, :], edgeT[:, bass.ds(g * GE, GE)]).then_inc(s_edge[k], 16)

                    def hand_over(k, turn, ek, eturn):
                        sp.wait_ge(s_gat[k], before[len(range(k, NG, RING))] + turn * (16 * TPG) + 16 * TPG)
                        if with_edges:
                            sp.wait_ge(s_edge[ek], eturn * 16 + 16)
                        sp.sem_inc(landed, 1)

                    def refill(g, k, ek, more):
                        end = sp.value_load(ends[0:1, bass.ds(g - LAG, 1)], min_val=1, max_val=NG * (nw + 1))
                        sp.wait_ge(done, end)
                        if more:
                            load_indices(g - LAG + RING, k)
                        if with_edges:
                            load_edges(g - LAG + ERING, ek)

                    before = {n: passes * (16 * TPG * n) if isinstance(passes, int) else sp.snap(passes * (16 * TPG * n))
                              for n in {len(range(k, NG, RING)) for k in range(RING)}}
                    for g in range(RING):
                        load_indices(g, g)
                    if with_edges:
                        for g in range(ERING):
                            load_edges(g, g)
                    for g in range(LAG):
                        hand_over(g, 0, g, 0)
                    LOOPS = (NG - RING) // RING
                    with sp.Fori(0, LOOPS) as i:
                        for u in range(RING):
                            k = LAG + u
                            hand_over(k % RING, i + k // RING, k % ERING, i * (RING // ERING) + k // ERING)
                            refill(i * RING + k, u, u % ERING, True)
                    for g in range(LAG + LOOPS * RING, NG):
                        hand_over(g % RING, g // RING, g % ERING, g // ERING)
                        if g - LAG + RING < NG or with_edges and g - LAG + ERING < NG:
                            refill(g, (g - LAG) % RING, (g - LAG) % ERING, g - LAG + RING < NG)

                @block.gpsimd
                def _(pool):
                    def gather(k, turn):
                        pool.wait_ge(s_idx[k], turn * 16 + 16)
                        pool.sem_inc(begun, 1)
                        for j in range(TPG):
                            pool.indirect_dma_start(rows[:, k, j, 0:width], None, table,
                                                    bass.IndirectOffsetOnAxis(ap=idx[:, k, j:j + 1], axis=0)).then_inc(s_gat[k], 16)
                    with pool.Fori(0, NG // RING) as i:
                        for k in range(RING):
                            gather(k, i)
                    for k in range(NG % RING):
                        gather(k, NG // RING)

                def engine_program(eng, stages, fields):
                    pairs = SURE + eng.value_load(ctl[0:1, pairs_at:pairs_at + 1], min_val=NG // 2 - SURE, max_val=max_pairs - SURE)

                    def one(q, par, have):
                        known = {}
                        for stage, lag, fields in stages:
                            for f in fields:
                                if have(lag) and (lag, f) not in known:
                                    known[lag, f] = eng.value_load(steps[bass.ds(q - lag, 1), f:f + 1], min_val=0,
                                                                   max_val=(nw, NG - 1, RING - 1, ERING - 1)[f])
                        for stage, lag, fields in stages:
                            if have(lag):
                                stage(q - lag, (par - lag) % 2, lambda f, lag=lag: known[lag, f])

                    for q in range(4):
                        one(q, q, lambda lag: lag <= q)
                    with eng.Fori(2, pairs) as i:
                        for par in range(2):
                            one(2 * i + par, par, lambda lag: True)
                    for k in range(3):
                        one(2 * pairs + k, k, lambda lag: lag > k)

                @block.vector
                def _(dve):
                    engine_program(dve, emit.vector(dve), None)

                @block.scalar
                def _(act):
                    act.preload_act_table(ACT.Exp)
                    engine_program(act, emit.scalar(act), None)

                @block.tensor
                def _(pe):
                    engine_program(pe, emit.tensor(pe), None)

        shared = {f"{n}{k}": sem(f"{n}{k}") for n in ("idx", "gat", "edge") for k in range(RING)}
        shared |= {n: sem(n) for n in ("landed", "begun", "done")}
        cleared = [v for n, v in shared.items() if not n.startswith("gat")]
        step_sems = {n: sem(n) for n in (
            "eq_ready", "eqt_ready", "eqts_ready", "u_ready", "ut_ready", "pre_ready", "v_ready", "relu_done",
            "rr_ready", "s_ready")}

        eq = work[:, 0:2 * TPG * P].rearrange("p (s j n) -> p s j n", s=2, j=TPG)
        eqT = work[:, 2048:2048 + TPG * P].rearrange("p (j n) -> p j n", j=TPG)
        uT = work[0:D, 3072:3072 + GE]
        vsum = work[:, 4096:4096 + TPG * D].rearrange("p (j c) -> p j c", j=TPG)
        rr = work[:, 5120:5120 + TPG * MW].rearrange("p (j c) -> p j c", j=TPG)
        dst3 = dstf[:].rearrange("p (g j) -> p g j", j=TPG)

        class Message:
            sems = shared

            @staticmethod
            def vector(dve):
                s = step_sems

                def accumulate(k, par, rec):
                    dve.wait_ge(s["s_ready"], k + 1)
                    if not (isinstance(k, int) and k == 0):
                        dve.wait_ge(shared["done"], k)
                    a = acc_m[:, bass.ds(rec(0), 1), :].rearrange("p w c -> p (w c)")
                    dve.tensor_tensor(a, a, ps[:, 6 + par, 0:MW], ALU.add).then_inc(shared["done"], 1)

                def match(q, par, rec):
                    dve.wait_ge(shared["landed"], rec(1) + 1)
                    d = dst3[:, bass.ds(rec(1), 1), :].rearrange("p g j -> p (g j)").unsqueeze(2).broadcast_to([P, TPG, WM])
                    dve.scalar_tensor_tensor(eq[:, par], d, base_m[:, bass.ds(rec(0), 1)],
                                             iota[:, 0:WM].unsqueeze(1).broadcast_to([P, TPG, WM]),
                                             ALU.subtract, ALU.is_equal).then_inc(s["eq_ready"], 1)

                def add_source(k, par, rec):
                    dve.wait_ge(s["pre_ready"], k + 1)
                    if not (isinstance(k, int) and k == 0):
                        dve.wait_ge(s["rr_ready"], k)
                    for half in range(2):
                        j0 = half * TPG // 2
                        ins = dve.tensor_tensor(
                            vsum[:, j0:j0 + TPG // 2, :],
                            ps[:, 4 + half, 0:TPG // 2 * D].rearrange("p (j c) -> p j c", c=D),
                            rows[:, bass.ds(rec(2), 1), j0:j0 + TPG // 2, 0:D].rearrange("p r j c -> p (r j) c"), ALU.add)
                    ins.then_inc(s["v_ready"], 1)
                return [(accumulate, 2, (0,)), (match, 0, (0, 1)), (add_source, 1, (2,))]

            @staticmethod
            def scalar(act):
                s = step_sems

                def copy_match(q, par, rec):
                    act.wait_ge(s["eqt_ready"], q + 1)
                    if not (isinstance(q, int) and q == 0):
                        act.wait_ge(s["pre_ready"], q)
                    nc.scalar.activation(eqT, ps[:, 0:2, :].rearrange("p b (j n) -> p (b j) n", n=P), ACT.Copy).then_inc(s["eqts_ready"], 1)

                def edge_relu(q, par, rec):
                    act.wait_ge(s["u_ready"], q + 1)
                    nc.scalar.activation(uT, ps[0:D, 2:4, :].rearrange("p b n -> p (b n)"), ACT.Relu, bias=cols[:, 3:4]).then_inc(s["ut_ready"], 1)

                def message_relu(k, par, rec):
                    act.wait_ge(s["v_ready"], k + 1)
                    if not (isinstance(k, int) and k == 0):
                        act.wait_ge(s["s_ready"], k)
                    nc.scalar.activation(rr[:, :, 0:D], vsum, ACT.Relu).then_inc(s["relu_done"], 1)
                    act.wait_ge(s["relu_done"], k + 1)
                    nc.scalar.activation(rr[:, :, D:2 * D], rr[:, :, 0:D], ACT.Square).then_inc(s["rr_ready"], 1)
                return [(copy_match, 0, ()), (edge_relu, 0, ()), (message_relu, 1, ())]

            @staticmethod
            def tensor(pe):
                s = step_sems

                def turn_match(q, par, rec):
                    pe.wait_ge(s["eq_ready"], q + 1)
                    if not (isinstance(q, int) and q == 0):
                        pe.wait_ge(s["eqts_ready"], q)
                    for j in range(TPG):
                        last = pe.transpose(ps[:, j // 4, (j % 4) * P:(j % 4 + 1) * P], eq[:, par, j, :], ident[:])
                    last.then_inc(s["eqt_ready"], 1)

                def edge_product(q, par, rec):
                    pe.wait_ge(shared["landed"], rec(1) + 1)
                    if not (isinstance(q, int) and q == 0):
                        pe.wait_ge(s["ut_ready"], q)
                    for half in range(2):
                        last = pe.matmul(bank(2 + half, D, 512), wt["We"][:],
                                         edge_ring[:, bass.ds(rec(3), 1), half * 512:(half + 1) * 512].rearrange("p r n -> p (r n)"),
                                         start=True, stop=True)
                    last.then_inc(s["u_ready"], 1)

                def message_product(k, par, rec):
                    pe.wait_ge(s["eqts_ready"], k + 1)
                    pe.wait_ge(s["ut_ready"], k + 1)
                    if not (isinstance(k, int) and k == 0):
                        pe.wait_ge(s["v_ready"], k)
                    ut = uT.rearrange("p (e j) -> p j e", j=TPG)
                    b_w = b_rows[:, bass.ds(rec(0), 1), :].rearrange("p w c -> p (w c)")
                    for j in range(TPG):
                        o = ps[:, 4 + j // 4, (j % 4) * D:(j % 4 + 1) * D]
                        pe.matmul(o, ut[:, j, :], W3s[:], start=True, stop=False)
                        last = pe.matmul(o, eqT[:, j, :], b_w, start=False, stop=True)
                    last.then_inc(s["pre_ready"], 1)

                def node_sums(k, par, rec):
                    pe.wait_ge(s["rr_ready"], k + 1)
                    if not (isinstance(k, int) and k < 2):
                        pe.wait_ge(shared["done"], k - 1)
                    for j in range(TPG):
                        last = pe.matmul(ps[:, 6 + par, 0:MW], eq[:, par, j, :], rr[:, j, :], start=(j == 0), stop=(j == TPG - 1))
                    last.then_inc(s["s_ready"], 1)
                return [(edge_product, 0, (1, 3)), (node_sums, 2, ()), (turn_match, 0, ()), (message_product, 1, (0,))]

        with nc.Block() as block:
            @block.vector
            def _(dve):
                dve.memset(rr[:, :, 2 * D:MW], 1.0)
        edge_block(steps_m, ends_m, 0, ROWS_M // 2, NWM, table_m, D, True, Message, 0)

        s_pe3 = sem("s_pe3")
        s_asked = sem("s_asked")
        s_rooted = sem("s_rooted")
        s_xt = sem("s_xt")
        s_d3 = sem("s_d3")
        s_v3 = sem("s_v3")
        s_add = sem("s_add")

        def layer_norm(dve, link, asked, rooted, value):
            for t in range(NT):
                last = dve.bn_stats(lnst[:, t, :], xn[:, t, :])
            link(last)
            for t in range(NT):
                last = dve.bn_aggr(lnmv[:, t, :], lnst[:, t, :])
            link(last)
            dve.tensor_scalar(lnr[:], lnmv[:, :, 1], EPS, None, ALU.add).then_inc(asked, 1)
            dve.wait_ge(rooted, value)
            link(dve.reciprocal(lnr[:], lnr[:]))
            for t in range(NT):
                last = dve.tensor_scalar(xn[:, t, :], xn[:, t, :], lnmv[:, t, 0:1], lnr[:, t:t + 1], ALU.subtract, ALU.mult)
            return last

        with nc.Block() as block:
            @block.tensor
            def _(pe):
                pe.matmul(ps[:, 1, 0:2 * D], ones[0:1, :], rowsb[0:1, 1:3, :].rearrange("p k c -> p (k c)"),
                          start=True, stop=True)
                pe.wait_ge(s_d3, 1)
                for t in range(NT):
                    last = pe.matmul(ps[:, 0, 0:2 * D], ones[:], acc_m[:, t, 0:2 * D], start=(t == 0), stop=(t == NT - 1))
                last.then_inc(s_pe3, 1)
                pe.wait_ge(s_v3, 1)
                for b, ts in enumerate(tiles):
                    if b >= 2:
                        pe.wait_ge(s_add, b - 1)
                    for t in ts:
                        last = pe.transpose(ps[:, 2 + b % 2, (t - ts[0]) * D:(t - ts[0] + 1) * D],
                                            nfT[:, t * P:(t + 1) * P], ident[0:D, 0:D])
                    last.then_inc(s_pe3, 1)
                pe.wait_ge(s_v3, 2)
                for b, ts in enumerate(tiles):
                    if b >= 2:
                        pe.wait_ge(s_xt, b - 1)
                    for t in ts:
                        last = pe.transpose(ps[0:D, 4 + b % 2, (t - ts[0]) * P:(t - ts[0] + 1) * P], xn[:, t, :], ident[:])
                    last.then_inc(s_pe3, 1)

            @block.scalar
            def _(act):
                act.wait_ge(s_asked, 1)
                nc.scalar.activation(rowsb[:, 4, :], rowsb[:, 4, :], ACT.Sqrt).then_inc(s_rooted, 1)
                act.wait_ge(s_asked, 2)
                nc.scalar.activation(small[0:D, 44:46], small[0:D, 42:44], ACT.Sqrt).then_inc(s_rooted, 1)
                act.wait_ge(s_asked, 3)
                nc.scalar.activation(lnr[:], lnr[:], ACT.Sqrt).then_inc(s_rooted, 1)
                for b, ts in enumerate(tiles):
                    act.wait_ge(s_pe3, 1 + NB + b + 1)
                    nc.scalar.activation(XT[0:D, ts[0] * P:(ts[-1] + 1) * P], ps[0:D, 4 + b % 2, 0:len(ts) * P],
                                         ACT.Copy).then_inc(s_xt, 1)

            @block.vector
            def _(dve):
                n = 1

                def link(ins):
                    nonlocal n
                    n += 1
                    ins.then_inc(s_d3, 1)
                    dve.wait_ge(s_d3, n)

                dve.tensor_scalar(acc_m[:, NT - 1, :], acc_m[:, NT - 1, :], rowmask[:, 0:1], None, ALU.mult).then_inc(s_d3, 1)
                dve.wait_ge(s_d3, 1)
                for b in range(NB):
                    m = min(512, N - b * 512)
                    last = dve.bn_stats(lnst[0:D, b, :], nfT[:, b * 512:b * 512 + m])
                link(last)
                link(dve.bn_aggr(small[0:D, 42:44], lnst[0:D, 0:NB, :].rearrange("p n s -> p (n s)")))
                link(dve.tensor_copy(small[0:D, 46:47], small[0:D, 42:43]))
                dve.wait_ge(s_pe3, 1)
                link(dve.tensor_copy(rowsb[:, 6:8, :], ps[:, 1, 0:2 * D].rearrange("p (k c) -> p k c", k=2)))
                link(dve.tensor_scalar(rowsb[:, 3:5, :], ps[:, 0, 0:2 * D].rearrange("p (k c) -> p k c", k=2), 1.0 / E, None, ALU.mult))
                link(dve.tensor_tensor(rowsb[:, 5, :], rowsb[:, 3, :], rowsb[:, 3, :], ALU.mult))
                link(dve.tensor_tensor(rowsb[:, 4, :], rowsb[:, 4, :], rowsb[:, 5, :], ALU.subtract))
                dve.tensor_scalar(rowsb[:, 4, :], rowsb[:, 4, :], 0.0, EPS, ALU.max, ALU.add).then_inc(s_asked, 1)
                dve.wait_ge(s_rooted, 1)
                link(dve.reciprocal(rowsb[:, 4, :], rowsb[:, 4, :]))
                link(dve.tensor_tensor(rowsb[:, 4, :], rowsb[:, 4, :], rowsb[:, 6, :], ALU.mult))
                link(dve.tensor_tensor(rowsb[:, 5, :], rowsb[:, 3, :], rowsb[:, 4, :], ALU.mult))
                link(dve.tensor_tensor(rowsb[:, 5, :], rowsb[:, 7, :], rowsb[:, 5, :], ALU.subtract))
                dve.tensor_scalar(small[0:D, 42:44], small[0:D, 42:44], EPS, None, ALU.add).then_inc(s_asked, 1)
                dve.wait_ge(s_rooted, 2)
                link(dve.reciprocal(small[0:D, 44:45], small[0:D, 45:46]))
                link(dve.tensor_tensor(small[0:D, 44:45], small[0:D, 44:45], cols[:, 1:2], ALU.mult))
                link(dve.tensor_tensor(small[0:D, 47:48], small[0:D, 46:47], small[0:D, 44:45], ALU.mult))
                link(dve.tensor_tensor(small[0:D, 47:48], cols[:, 2:3], small[0:D, 47:48], ALU.subtract))
                dve.tensor_scalar(nfT, nfT, small[0:D, 44:45], small[0:D, 47:48], ALU.mult, ALU.add).then_inc(s_v3, 1)
                sums, spare, degree = acc_m[:, 0:NT, 0:D], acc_m[:, 0:NT, D:2 * D], acc_m[:, 0:NT, 2 * D:MW]
                dve.tensor_tensor(sums, sums, rowsb[:, 4, :].unsqueeze(1).broadcast_to([P, NT, D]), ALU.mult)
                link(dve.tensor_tensor(spare, degree.broadcast_to([P, NT, D]), rowsb[:, 5, :].unsqueeze(1).broadcast_to([P, NT, D]), ALU.mult))
                link(dve.tensor_tensor(sums, sums, spare, ALU.add))
                link(dve.tensor_tensor(xn[:], xn[:], sums, ALU.add))
                for b, ts in enumerate(tiles):
                    dve.wait_ge(s_pe3, 1 + b + 1)
                    a = xn[:, ts[0]:ts[-1] + 1, :]
                    last = dve.tensor_tensor(a, a, ps[:, 2 + b % 2, 0:len(ts) * D].rearrange("p (t c) -> p t c", c=D), ALU.add)
                    last.then_inc(s_add, 1)
                dve.wait_ge(s_add, NB)
                layer_norm(dve, link, s_asked, s_rooted, 3).then_inc(s_v3, 1)

        acc = big[:]
        ad = lnst[:].rearrange("p t s -> p (t s)")[:, 0:NWA + 1]
        stage = work[:, 0:NT * TW].rearrange("p (t c) -> p t c", c=TW)
        negmax = sb("negmax", [P, NWA + 1])
        rden = sb("rden", [P, NWA])
        ne = work[:, 7168:7168 + TPG * WA].rearrange("p (j n) -> p j n", j=TPG)
        masked = work[:, 0:2048].rearrange("p (s j h n) -> p s j h n", s=2, j=TPG, h=H)
        positive = work[:, 2048:3072]
        logit = work[:, 7424:9472].rearrange("p (s n) -> p s n", s=2)
        prob = work[:, 3072:5120].rearrange("p (s j e) -> p s j e", s=2, j=TPG)
        probT = work[:, 5120:7168].rearrange("p (s j e) -> p s j e", s=2, j=TPG)
        locmax, neg, keep = (small[:, 48 + 2 * k:50 + 2 * k] for k in range(3))
        a_sems = {n: sem(n) for n in (
            "ne_ready", "a_ready", "t_ready", "positive_ready", "max_ready", "neg_ready", "keep_ready",
            "saved", "p_ready", "pt_ready", "pts_ready", "o_ready", "paced", "turned")}

        class Attention:
            sems = shared

            @staticmethod
            def vector(dve):
                s = a_sems

                def accumulate(k, par, rec):
                    dve.wait_ge(s["o_ready"], k + 1)
                    if not (isinstance(k, int) and k == 0):
                        dve.wait_ge(shared["done"], k)
                    a = acc[:, bass.ds(rec(0), 1), :].rearrange("p w c -> p (w c)")
                    dve.scalar_tensor_tensor(a, a, keep[:, par:par + 1], ps[:, 6 + par, 0:D + 1], ALU.mult, ALU.add).then_inc(shared["done"], 1)

                def maximum(k, par, rec):
                    dve.wait_ge(s["positive_ready"], k + 1)
                    if not (isinstance(k, int) and k < 2):
                        dve.wait_ge(s["p_ready"], k - 1)
                    dve.sem_inc(s["turned"], 1)
                    dve.tensor_tensor_reduce(out=logit[:, par], in0=positive, in1=ps[:, 2 * par:2 * par + 2, :].rearrange("p b n -> p (b n)"),
                                             scale=SLOPE, scalar=3 * MASKED, op0=ALU.add, op1=ALU.max,
                                             accum_out=locmax[:, par:par + 1]).then_inc(s["max_ready"], 1)

                def mask(q, par, rec):
                    dve.wait_ge(shared["landed"], rec(1) + 1)
                    d = dst3[:, bass.ds(rec(1), 1), :].rearrange("p g j -> p (g j)").unsqueeze(2).broadcast_to([P, TPG, WA])
                    if not (isinstance(q, int) and q == 0):
                        dve.wait_ge(s["a_ready"], q)
                    dve.scalar_tensor_tensor(ne, d, base_a[:, bass.ds(rec(0), 1)],
                                             iota[:, 0:WA].unsqueeze(1).broadcast_to([P, TPG, WA]),
                                             ALU.subtract, ALU.not_equal).then_inc(s["ne_ready"], 1)
                    dve.wait_ge(s["ne_ready"], q + 1)
                    for h in range(H):
                        source = rows[:, bass.ds(rec(2), 1), :, D + 1 + h].rearrange("p r j -> p (r j)").unsqueeze(2).broadcast_to([P, TPG, WA])
                        last = dve.scalar_tensor_tensor(masked[:, par, :, h, :], ne, MASKED, source, ALU.mult, ALU.add)
                    last.then_inc(s["a_ready"], 1)

                def running(k, par, rec):
                    dve.wait_ge(s["max_ready"], k + 1)
                    if not (isinstance(k, int) and k == 0):
                        dve.wait_ge(s["saved"], k)
                    dve.scalar_tensor_tensor(neg[:, par:par + 1], locmax[:, par:par + 1], -1.0, negmax[:, bass.ds(rec(0), 1)],
                                             ALU.mult, ALU.min).then_inc(s["neg_ready"], 1)
                return [(accumulate, 3, (0,)), (mask, 0, (0, 1, 2)), (maximum, 1, ()), (running, 1, (0,))]

            @staticmethod
            def scalar(act):
                s = a_sems

                def positives(k, par, rec):
                    act.wait_ge(s["t_ready"], k + 1)
                    if not (isinstance(k, int) and k == 0):
                        act.wait_ge(s["max_ready"], k)
                    act.sem_inc(s["paced"], 1)
                    nc.scalar.activation(positive, ps[:, 2 * par:2 * par + 2, :].rearrange("p b n -> p (b n)"), ACT.Relu,
                                         bias=ad[:, bass.ds(rec(0), 1)], scale=GAIN).then_inc(s["positive_ready"], 1)

                def copy_probs(k, par, rec):
                    act.wait_ge(s["pt_ready"], k + 1)
                    if not (isinstance(k, int) and k < 2):
                        act.wait_ge(s["o_ready"], k - 1)
                    nc.scalar.activation(probT[:, par], ps[:, 4:6, :].rearrange("p b (j n) -> p (b j) n", n=P), ACT.Copy).then_inc(s["pts_ready"], 1)

                def exponentials(k, par, rec):
                    act.wait_ge(s["neg_ready"], k + 1)
                    if not (isinstance(k, int) and k < 2):
                        act.wait_ge(shared["done"], k - 1)
                    if not (isinstance(k, int) and k == 0):
                        act.wait_ge(s["saved"], k)
                    w = rec(0)
                    act.sem_inc(s["paced"], 1)
                    nc.scalar.activation(keep[:, par:par + 1], negmax[:, bass.ds(w, 1)], ACT.Exp, bias=neg[:, par:par + 1],
                                         scale=-1.0).then_inc(s["keep_ready"], 1)
                    nc.scalar.activation(prob[:, par].rearrange("p j e -> p (j e)"), logit[:, par], ACT.Exp, bias=neg[:, par:par + 1]).then_inc(s["p_ready"], 1)
                    act.wait_ge(s["keep_ready"], k + 1)
                    act.sem_inc(s["turned"], 1)
                    nc.scalar.activation(negmax[:, bass.ds(w, 1)], neg[:, par:par + 1], ACT.Copy).then_inc(s["saved"], 1)
                return [(positives, 1, (0,)), (copy_probs, 2, ()), (exponentials, 1, (0,))]

            @staticmethod
            def tensor(pe):
                s = a_sems

                def turn_probs(k, par, rec):
                    pe.wait_ge(s["p_ready"], k + 1)
                    if not (isinstance(k, int) and k == 0):
                        pe.wait_ge(s["pts_ready"], k)
                    for j in range(TPG):
                        last = pe.transpose(ps[:, 4 + j // 4, (j % 4) * P:(j % 4 + 1) * P], prob[:, par, j, :], ident[:])
                    last.then_inc(s["pt_ready"], 1)

                def turn_mask(q, par, rec):
                    pe.wait_ge(s["a_ready"], q + 1)
                    if not (isinstance(q, int) and q < 2):
                        pe.wait_ge(s["max_ready"], q - 1)
                    for j in range(TPG):
                        last = pe.transpose(ps[:, 2 * par + j // 4, (j % 4) * P:(j % 4 + 1) * P],
                                            masked[:, par, j].rearrange("p h n -> p (h n)"), ident[:])
                    last.then_inc(s["t_ready"], 1)

                def weighted_sums(k, par, rec):
                    pe.wait_ge(s["pts_ready"], k + 1)
                    if not (isinstance(k, int) and k < 2):
                        pe.wait_ge(shared["done"], k - 1)
                    for j in range(TPG):
                        last = pe.matmul(ps[:, 6 + par, 0:D + 1], probT[:, par, j, :],
                                         rows[:, bass.ds(rec(2), 1), j, 0:D + 1].rearrange("p r c -> p (r c)"),
                                         start=(j == 0), stop=(j == TPG - 1))
                    last.then_inc(s["o_ready"], 1)
                return [(turn_probs, 2, ()), (turn_mask, 0, ()), (weighted_sums, 2, (2,))]

        s_wl = sem("s_wl")
        s_lt = sem("s_lt")
        s_lc = sem("s_lc")
        s_ad = sem("s_ad")
        s_ta = sem("s_ta")
        s_r = sem("s_r")
        s_m1 = sem("s_m1")
        s_m2 = sem("s_m2")
        s_fo = sem("s_fo")
        s_x = sem("s_x")
        WPB = 512 // WA
        WB = -(-NWA // WPB)
        windows = [(b * WPB, min(NWA, b * WPB + WPB)) for b in range(WB)]
        half = [(4 * b, min(NT, 4 * b + 4)) for b in range(NB)]

        with nc.Block() as block:
            @block.gpsimd
            def _(pool):
                for v in cleared:
                    pool.sem_clear(v)

        with nc.Fori(0, LAYERS) as l:
            with nc.Block() as block:
                @block.vector
                def _(dve):
                    dve.tensor_copy(w_l[:], w_all[:, bass.ds(l, 1), :].rearrange("p l c -> p (l c)"))
                    dve.tensor_copy(z_l[:], z_all[:, bass.ds(l, 1), :].rearrange("p l c -> p (l c)"))
                    dve.tensor_copy(bias_l[:], bias_all[:, bass.ds(l, 1)]).then_inc(s_wl, 1)
                    dve.memset(negmax[:], FLOOR)
                    dve.memset(ad[:, NWA:NWA + 1], 0.0)
                    for b, ts in enumerate(tiles):
                        if b % 2 == 0:
                            dve.wait_ge(s_lt, b + 1)
                            dve.tensor_copy(stage[:, ts[0]:ts[-1] + 1, :],
                                            ps[:, b % 4, 0:len(ts) * TW].rearrange("p (t c) -> p t c", c=TW)).then_inc(s_lc, 1)
                    dve.wait_ge(s_ad, 1)
                    dve.tensor_scalar(ad[:, 0:NWA], ps[:, 4, 0:NWA], GAIN, None, ALU.mult)

                @block.gpsimd
                def _(pool):
                    pool.memset(acc, 0.0)

                @block.tensor
                def _(pe):
                    pe.wait_ge(s_wl, 1)
                    for b, ts in enumerate(tiles):
                        if b >= 4:
                            pe.wait_ge(s_lc if b % 2 == 0 else s_m1, (b - 4) // 2 + 1)
                        for t in ts:
                            last = pe.matmul(ps[:, b % 4, (t - ts[0]) * TW:(t - ts[0] + 1) * TW], XT[:, t * P:(t + 1) * P], w_l[:],
                                             start=True, stop=True)
                        last.then_inc(s_lt, 1)
                    xv = XT[0:D, :].rearrange("p (w n) -> p n w", n=WA)
                    for n in range(WA):
                        last = pe.matmul(ps[:, 4, 0:NWA], z_l[:, WA - 1 - n:WA - 1 - n + P], xv[:, n, :],
                                         start=(n == 0), stop=(n == WA - 1))
                    last.then_inc(s_ad, 1)

                @block.scalar
                def _(act):
                    for b, ts in enumerate(tiles):
                        if b % 2 == 1:
                            act.wait_ge(s_lt, b + 1)
                            nc.scalar.activation(stage[:, ts[0]:ts[-1] + 1, :],
                                                 ps[:, b % 4, 0:len(ts) * TW].rearrange("p (t c) -> p t c", c=TW), ACT.Copy).then_inc(s_m1, 1)

                @block.sync
                def _(sp):
                    sp.wait_ge(s_lc, (NB + 1) // 2)
                    sp.wait_ge(s_m1, NB // 2)
                    sp.dma_start(table_a.rearrange("(t p) c -> p t c", p=P), stage).then_inc(s_ta, 16)
                    sp.wait_ge(s_ta, 16)

            edge_block(steps_a, ends_a, 2, ROWS_A // 2, NWA, table_a, TW, False, Attention, l + 1)

            with nc.Block() as block:
                @block.vector
                def _(dve):
                    dve.tensor_scalar(rden[:], acc[:, 0:NWA, D], 1e-16, None, ALU.add).then_inc(s_r, 1)
                    dve.wait_ge(s_r, 1)
                    dve.reciprocal(rden[:], rden[:]).then_inc(s_r, 1)
                    dve.wait_ge(s_r, 2)
                    for b, (w0, w1) in enumerate(windows):
                        a = acc[:, w0:w1, 0:D]
                        dve.tensor_tensor(a, a, rden[:, w0:w1].unsqueeze(2).broadcast_to([P, w1 - w0, D]), ALU.mult).then_inc(s_r, 1)
                        dve.wait_ge(s_r, 3 + b)
                        dve.tensor_tensor(a, a, headmask[:].unsqueeze(1).broadcast_to([P, w1 - w0, D]), ALU.mult).then_inc(s_m2, 1)

                @block.tensor
                def _(pe):
                    for b, (w0, w1) in enumerate(windows):
                        pe.wait_ge(s_m2, b + 1)
                        if b >= 4:
                            pe.wait_ge(s_x, b - 3)
                        for w in range(w0, w1):
                            last = pe.matmul(ps[0:D, b % 4, (w - w0) * WA:(w - w0 + 1) * WA], acc[:, w, 0:D], fold[:], start=True, stop=True)
                        last.then_inc(s_fo, 1)

                @block.scalar
                def _(act):
                    for b, (w0, w1) in enumerate(windows):
                        act.wait_ge(s_fo, b + 1)
                        nc.scalar.activation(XT[0:D, w0 * WA:w1 * WA], ps[0:D, b % 4, 0:(w1 - w0) * WA], ACT.Relu,
                                             bias=bias_l[:, 0:1]).then_inc(s_x, 1)

            with nc.Block() as block:
                @block.gpsimd
                def _(pool):
                    for v in (*cleared, *a_sems.values(), s_wl, s_lt, s_lc, s_ad, s_ta, s_r, s_m1, s_m2, s_fo, s_x):
                        pool.sem_clear(v)

        s_back = sem("s_back")
        s_res = sem("s_res")
        s_ask5 = sem("s_ask5")
        s_root5 = sem("s_root5")
        s_d5 = sem("s_d5")
        s_fin = sem("s_fin")
        s_out = sem("s_out")
        with nc.Block() as block:
            @block.tensor
            def _(pe):
                for b, ts in enumerate(tiles):
                    if b >= 4:
                        pe.wait_ge(s_res, b - 3)
                    for t in ts:
                        last = pe.transpose(ps[:, b % 4, (t - ts[0]) * D:(t - ts[0] + 1) * D], XT[0:D, t * P:(t + 1) * P], ident[0:D, 0:D])
                    last.then_inc(s_back, 1)

            @block.scalar
            def _(act):
                act.wait_ge(s_ask5, 1)
                nc.scalar.activation(lnr[:], lnr[:], ACT.Sqrt).then_inc(s_root5, 1)

            @block.vector
            def _(dve):
                n = 0

                def link(ins):
                    nonlocal n
                    n += 1
                    ins.then_inc(s_d5, 1)
                    dve.wait_ge(s_d5, n)

                for b, ts in enumerate(tiles):
                    dve.wait_ge(s_back, b + 1)
                    a = xn[:, ts[0]:ts[-1] + 1, :]
                    dve.tensor_tensor(a, a, ps[:, b % 4, 0:len(ts) * D].rearrange("p (t c) -> p t c", c=D), ALU.add).then_inc(s_res, 1)
                dve.wait_ge(s_res, NB)
                layer_norm(dve, link, s_ask5, s_root5, 1).then_inc(s_fin, 1)

            @block.sync
            def _(sp):
                sp.wait_ge(s_fin, 1)
                sp.dma_start(out[0:(NT - 1) * P, :].rearrange("(t p) c -> p t c", p=P), xn[:, 0:NT - 1, :]).then_inc(s_out, 16)
                sp.dma_start(out[(NT - 1) * P:N, :], xn[0:N - (NT - 1) * P, NT - 1, :]).then_inc(s_out, 16)
                sp.wait_ge(s_out, 32)


_RENAME = dict(
    Wn="L0_gnn_W_node", bn="L0_gnn_b_node", gn="L0_gnn_g_node", betan="L0_gnn_beta_node",
    We="L0_gnn_W_edge", be="L0_gnn_b_edge", ge="L0_gnn_g_edge", betae="L0_gnn_beta_edge",
    Wm="L0_gnn_W_msg", bm="L0_gnn_b_msg", gm="L0_gnn_g_msg", betam="L0_gnn_beta_msg",
    Wl="L1_gnn_W", att_src="L1_gnn_att_src", att_dst="L1_gnn_att_dst", bias="L1_gnn_bias")
_ORDER = ["x", "xT", "src", "dst", "edgeT", "Wn", "bn", "gn", "betan", "We", "be", "ge", "betae",
          "Wm", "bm", "gm", "betam", "Wl", "WlT", "att_src", "att_dst", "bias"]


def kernel(**inputs):
    import numpy as _np
    import concourse.bacc as _bacc
    from concourse import mybir as _mybir
    from concourse.bass_utils import run_bass_kernel_spmd as _run

    given = {k: _np.ascontiguousarray(inputs[v]) for k, v in _RENAME.items()}
    x = _np.ascontiguousarray(inputs["x"])
    given["x"] = x
    given["xT"] = _np.concatenate([x.T, _np.zeros((D, NPAD - N), x.dtype)], axis=1)
    source, target = _np.asarray(inputs["src"]), _np.asarray(inputs["dst"])
    given["src"] = _np.concatenate([source, _np.zeros(EPAD - E, source.dtype)])
    given["dst"] = _np.concatenate([target, _np.full(EPAD - E, NPAD - 1, target.dtype)])
    attr = _np.asarray(inputs["edge_attr_4"])
    given["edgeT"] = _np.concatenate([attr.T, _np.zeros((DE, EPAD - E), attr.dtype)], axis=1)
    given["WlT"] = _np.ascontiguousarray(_np.transpose(given["Wl"], (0, 2, 1)))

    nc = _bacc.Bacc("TRN2", target_bir_lowering=False, num_devices=1)
    arrays, args = {}, []
    for name in _ORDER:
        a = _np.ascontiguousarray(given[name])
        arrays[f"in_{name}_dram"] = a
        args.append(nc.dram_tensor(f"in_{name}_dram", a.shape, _mybir.dt.from_np(a.dtype), kind="ExternalInput").ap())
    args.append(nc.dram_tensor("out_0_dram", (N, D), _mybir.dt.float32, kind="ExternalOutput").ap())
    gnn_kernel(nc, *args)
    r = _run(nc, [arrays], core_ids=[0])
    return r.results[0]["out_0_dram"]
```

```python
from contextlib import ExitStack

import concourse.bass as bass
from concourse import mybir

ALU = mybir.AluOpType
ACT = mybir.ActivationFunctionType
AX = mybir.AxisListType
F32 = mybir.dt.float32
I32 = mybir.dt.int32

P = 128
N, E, D, DE = 6250, 206250, 96, 4
LAYERS, H = 3, 4
C = D // H
EPS = 1e-5
SLOPE = 0.2
GAIN = 1 / SLOPE - 1

TPG = 8
GE = P * TPG
NG = -(-E // GE)
EPAD = NG * GE
NT = -(-N // P)
NPAD = NT * P
RING = 8
ERING = 4
LAG = 3

WA = 32
NWA = NPAD // WA
WM = P
NWM = NPAD // WM

TW = D + 1 + H
ZW = WA - 1 + P
MW = 2 * D + 1
ROW_A = D + 4
ROW_M = MW + 1 + D

QUADS_A = [[("row", -3), ("row", -2), ("row", -1), ("row", 0)],
           [("row", 1), ("ready", 0), ("ready", 1), ("slot", 0)],
           [("slot", 1), ("slot", -2), ("slot", -1), None]]
QUADS_M = [[("row", -2), ("row", -1), ("row", 0), ("row", 1)],
           [("ready", 0), ("ready", 1), ("slot", -1), ("slot", 0)],
           [("ready", 0), ("ready", 1), ("eslot", 0), ("eslot", 1)]]
TOP = NWA * ROW_A
BACK, STEPS_AT = 3, 5
PAIRS_A = NG * NWA // 2 + 2
PAIRS_M = NG * NWM // 2 + 2
LIST_A = -(-PAIRS_A // P) * P
LIST_M = -(-PAIRS_M // P) * P

CH = 512
FULL = E // CH
SPAN = 8
SURE = 4
KG = -(-NG // P)

MASKED = -1e30
FLOOR = 1e20


def gnn_kernel(nc, x, xT, src, dst, edgeT, Wn, bn, gn, betan, We, be, ge, betae,
               Wm, bm, gm, betam, Wl, WlT, att_src, att_dst, bias, out):
    with ExitStack() as ctx:
        def sb(name, shape, dt=F32):
            return ctx.enter_context(nc.sbuf_tensor(name, shape, dt))

        def dram(name, shape, dt=F32):
            return nc.dram_tensor(name, shape, dt).ap()

        names = []

        def sem(name):
            names.append(name)
            return ctx.enter_context(nc.semaphore(name))

        table_m = dram("table_m", (NPAD, D))
        table_a = dram("table_a", (NPAD, TW))
        steps_a = dram("steps_a", (LIST_A, 16), I32)
        steps_m = dram("steps_m", (LIST_M, 16), I32)

        iota = sb("iota", [P, 2 * P])
        part = sb("part", [P, 1])
        part_i = sb("part_i", [P, 4], I32)
        ident = sb("ident", [P, P])
        fold = sb("fold", [P, WA])
        headmask = sb("headmask", [P, D])
        rowmask = sb("rowmask", [P, 1])
        ones = sb("ones", [P, P])
        dstf = sb("dstf", [P, (NG + 1) * TPG])
        ctl = sb("ctl", [1, 8], I32)
        ends_a = sb("ends_a", [1, NG], I32)
        ends_m = sb("ends_m", [1, NG], I32)
        idx = sb("idx", [P, RING, TPG], I32)
        rows = sb("rows", [P, RING, TPG, TW])
        XT = sb("XT", [D + 1, NPAD])
        xn = sb("xn", [P, NT, D])
        big = sb("big", [P, (NWA + 1) * ROW_A])
        w_all = sb("w_all", [D + 1, LAYERS, TW])
        z_all = sb("z_all", [D, LAYERS, ZW])
        bias_all = sb("bias_all", [D, LAYERS])
        w_l = sb("w_l", [D + 1, TW])
        z_l = sb("z_l", [D, ZW])
        bias_l = sb("bias_l", [D, 1])
        small = sb("small", [P, 64])
        rowsb = sb("rowsb", [P, 8, D])
        work = sb("work", [P, 9472])
        lnst = sb("lnst", [P, NT, 6])
        lnmv = sb("lnmv", [P, NT, 2])
        lnr = sb("lnr", [P, NT])

        ps = ctx.enter_context(nc.psum_tensor("ps", [P, 8, 512], F32))

        def bank(b, rows_, cols):
            return ps[0:rows_, b, 0:cols]

        s_load = sem("s_load")
        s_iota = sem("s_iota")
        s_const = sem("s_const")
        s_v = sem("s_v")
        s_a = sem("s_a")
        s_p = sem("s_p")
        s_q = sem("s_q")

        wt = dict(
            Wn=sb("sWn", [D, D]), W1=sb("sW1", [D, D]), W2=sb("sW2", [D, D]), W3=sb("sW3", [D, D]),
            We=sb("sWe", [DE, D]), cols=sb("cols", [D, 8]),
            WT=sb("sWT", [D, LAYERS, D]), att=sb("att", [D, LAYERS, 2 * H]),
        )
        cols = wt["cols"]
        W3s = sb("W3s", [D, D])
        LOADS = 13 + 2 * H

        def column(v):
            return v.rearrange("(c o) -> c o", o=1)

        def row(v):
            return v.rearrange("(o c) -> o c", o=1)

        with nc.Block() as block:
            @block.sync
            def _(sp):
                dsti = work[:, 0:NG * TPG].bitcast(I32)
                with nc.allow_non_contiguous_dma(reason="columns of channels"):
                    sp.dma_start(dsti.rearrange("p (g j) -> p g j", j=TPG),
                                 dst.rearrange("(g p j) -> p g j", p=P, j=TPG)).then_inc(s_load, 16)
                    sp.dma_start(XT[0:D, :], xT).then_inc(s_load, 16)
                    sp.dma_start(xn[:, 0:NT - 1, :], x[0:(NT - 1) * P, :].rearrange("(t p) c -> p t c", p=P)).then_inc(s_load, 16)
                    sp.dma_start(wt["Wn"][:], Wn).then_inc(s_load, 16)
                    for k in range(3):
                        sp.dma_start(wt[f"W{k + 1}"][:], Wm[k * D:(k + 1) * D, :]).then_inc(s_load, 16)
                    sp.dma_start(wt["We"][:], We).then_inc(s_load, 16)
                    sp.dma_start(wt["WT"][:], WlT.rearrange("l o i -> o l i")).then_inc(s_load, 16)
                    sp.dma_start(bias_all[:], bias.rearrange("l c -> c l")).then_inc(s_load, 16)
                    sp.dma_start(rowsb[0:1, 0, :], row(bm)).then_inc(s_load, 16)
                    for k, v in enumerate((bn, gn, betan, be, ge, betae)):
                        sp.dma_start(cols[:, k:k + 1], column(v)).then_inc(s_load, 16)
                    for k, v in enumerate((gm, betam)):
                        sp.dma_start(rowsb[0:1, 1 + k, :], row(v)).then_inc(s_load, 16)
                    sp.wait_ge(s_const, 1)
                    sp.dma_start(w_all[0:D, :, 0:D], Wl.rearrange("l i o -> i l o")).then_inc(s_load, 16)
                    sp.dma_start(xn[0:N - (NT - 1) * P, NT - 1, :], x[(NT - 1) * P:N, :]).then_inc(s_load, 16)
                    for h in range(H):
                        for k, v in enumerate((att_src, att_dst)):
                            sp.dma_start(wt["att"][h * C:(h + 1) * C, :, k * H + h:k * H + h + 1],
                                         v[:, h, :].rearrange("l (c o) -> c l o", o=1)).then_inc(s_load, 16)
            LOADED = 16 * (12 + 6 + 2 + 1 + 2 * H)

            @block.gpsimd
            def _(pool):
                pool.iota(iota[:], [[1, 2 * P]], base=0, channel_multiplier=0,
                          allow_small_or_imprecise_dtypes=True).then_inc(s_iota, 1)
                pool.iota(part[:], [[0, 1]], base=0, channel_multiplier=1,
                          allow_small_or_imprecise_dtypes=True).then_inc(s_iota, 1)
                pool.iota(part_i[:, 0:1], [[0, 1]], base=0, channel_multiplier=1).then_inc(s_iota, 1)
                pool.iota(headmask[:].rearrange("p (h c) -> p h c", c=C), [[1, H], [0, C]], base=0,
                          channel_multiplier=0, allow_small_or_imprecise_dtypes=True).then_inc(s_iota, 1)

            @block.vector
            def _(dve):
                dve.memset(wt["att"][:], 0.0)
                dve.memset(xn[:, NT - 1, :], 0.0)
                dve.memset(XT[D:D + 1, :], 1.0)
                dve.memset(w_all[:], 0.0)
                dve.memset(z_all[:], 0.0)
                dve.memset(ones[:], 1.0).then_inc(s_const, 1)
                dve.wait_ge(s_const, 1)
                dve.memset(w_all[D:D + 1, :, D:D + 1], 1.0)
                dve.wait_ge(s_iota, 4)
                dve.tensor_scalar(ident[:], iota[:, 0:P], part[:, 0:1], None, ALU.is_equal)
                dve.tensor_scalar(part_i[:, 1:2], part_i[:, 0:1], 5, None, ALU.arith_shift_right)
                dve.tensor_scalar(part_i[:, 2:3], part_i[:, 0:1], WA - 1, None, ALU.bitwise_and)
                dve.tensor_scalar(rowmask[:], part[:], float(N - (NT - 1) * P), None, ALU.is_lt).then_inc(s_const, 1)
                dve.wait_ge(s_const, 2)
                dve.tensor_copy(small[:, 0:2], part_i[:, 1:3]).then_inc(s_const, 1)
                dve.wait_ge(s_const, 3)
                dve.tensor_scalar(fold[:], iota[:, 0:WA], small[:, 1:2], None, ALU.is_equal)
                dve.tensor_scalar(headmask[:], headmask[:], small[:, 0:1], None, ALU.is_equal).then_inc(s_const, 1)
                dve.wait_ge(s_load, LOADED)
                dve.tensor_copy(dstf[:, TPG:], work[:, 0:NG * TPG].bitcast(I32)).then_inc(s_const, 1)
                dve.wait_ge(s_const, 5)

        def build_steps(tag, shift, nw, width, quads, steps, ends, pairs_at):
            lo_hi = small[:, 8:8 + 2 * KG]
            lo_hi_i = sb(f"lohi_{tag}", [P, 2 * KG], I32)
            gmm = work[:, 2048:2048 + 2 * NG].rearrange("p (k g) -> p k g", k=2)
            tri = work[:, 2560:2560 + KG * NG].rearrange("p (k g) -> p k g", k=KG)
            eye = work[:, 3072:3072 + KG * NG].rearrange("p (k g) -> p k g", k=KG)
            spread = work[:, 3584:3584 + KG * 2 * P].rearrange("p (k v m) -> p k v m", k=KG, v=2)
            endv = work[:, 4608:4608 + 2 * NG].rearrange("p (v g) -> p v g", v=2)
            hit = work[:, 5120:5120 + STEPS_AT * NG].rearrange("p (s g) -> p s g", s=STEPS_AT)
            got = work[:, 6144:6144 + 16]
            got_i = work[:, 6160:6176].bitcast(I32)
            of = {f: work[:, 6176 + 8 * k:6176 + 8 * k + STEPS_AT] for k, f in enumerate(
                ("q", "group", "window", "row", "ready", "slot", "eslot"))}
            slots_i = work[:, 6240:6240 + 2 * 8].bitcast(I32)
            s_red, s_tr, s_mm, s_ends, s_rec, s_sent, s_d, s_l = (
                sem(f"{n}_{tag}") for n in ("s_red", "s_tr", "s_mm", "s_ends", "s_rec", "s_sent", "s_d", "s_l"))
            sizes = [min(P, NG - k * P) for k in range(KG)]
            with nc.Block() as block:
                @block.vector
                def _(dve):
                    n = 0

                    def link(ins):
                        nonlocal n
                        n += 1
                        ins.then_inc(s_d, 1)
                        dve.wait_ge(s_d, n)

                    view = dstf[:, TPG:].rearrange("p (g j) -> p g j", j=TPG)
                    dve.tensor_reduce(gmm[:, 0, :], view, AX.X, ALU.min)
                    dve.tensor_reduce(gmm[:, 1, :], view, AX.X, ALU.max).then_inc(s_red, 1)
                    link(dve.memset(lo_hi, 0.0))
                    for k in range(KG):
                        link(dve.tensor_scalar(small[:, 20:21], part[:], float(k * P), None, ALU.add))
                        dve.tensor_scalar(tri[:, k, :], iota[:, 0:NG], small[:, 20:21], None, ALU.is_ge)
                        link(dve.tensor_scalar(eye[:, k, :], iota[:, 0:NG], small[:, 20:21], None, ALU.is_equal))
                    dve.wait_ge(s_tr, 1)
                    for k in range(KG):
                        m = sizes[k]
                        dve.tensor_reduce(lo_hi[0:m, k:k + 1], ps[0:m, k, 0:P], AX.X, ALU.min)
                        link(dve.tensor_reduce(lo_hi[0:m, KG + k:KG + k + 1], ps[0:m, k, P:2 * P], AX.X, ALU.max))
                    link(dve.tensor_copy(lo_hi_i[:], lo_hi))
                    link(dve.tensor_scalar(lo_hi_i[:], lo_hi_i[:], shift, None, ALU.arith_shift_right))
                    link(dve.tensor_copy(lo_hi, lo_hi_i[:]))
                    link(dve.tensor_scalar(lo_hi[:, KG:], lo_hi[:, KG:], 1.0, None, ALU.add))
                    link(dve.tensor_tensor(lo_hi[:, 0:KG], lo_hi[:, KG:], lo_hi[:, 0:KG], ALU.subtract))
                    for k in range(KG):
                        dve.tensor_scalar(spread[:, k, 0, :], ones[:], lo_hi[:, k:k + 1], None, ALU.mult)
                        last = dve.tensor_scalar(spread[:, k, 1, :], ones[:], lo_hi[:, KG + k:KG + k + 1], None, ALU.mult)
                    last.then_inc(s_red, 1)
                    dve.wait_ge(s_mm, 1)
                    link(dve.tensor_copy(endv[:, 0, :], ps[:, 2, 0:NG]))
                    link(dve.tensor_tensor(endv[:, 1, :], ps[:, 3, 0:NG], endv[:, 0, :], ALU.subtract))
                    dve.tensor_copy(ends[:], endv[0:1, 0, :]).then_inc(s_ends, 1)
                    dve.wait_ge(s_ends, 1)
                    dve.tensor_copy(small[0:1, 24:25], ends[0:1, NG - 1:NG]).then_inc(s_ends, 1)
                    dve.wait_ge(s_ends, 2)
                    link(dve.tensor_scalar(small[0:1, 25:26], small[0:1, 24:25], 3.0, None, ALU.add))
                    link(dve.tensor_scalar(small[0:1, 24:25], small[0:1, 24:25], 1.0 - 2 * SURE, None, ALU.add))
                    link(dve.tensor_copy(ctl[0:1, 6:8], small[0:1, 24:26]))
                    dve.tensor_scalar(ctl[0:1, pairs_at:pairs_at + 1], ctl[0:1, 6:7], 1, None, ALU.arith_shift_right)
                    link(dve.tensor_scalar(ctl[0:1, 5:6], ctl[0:1, 7:8], 8, None, ALU.arith_shift_right))
                    link(dve.tensor_copy(small[0:1, 25:26], ctl[0:1, 5:6]))
                    link(dve.tensor_scalar(small[0:1, 25:26], small[0:1, 25:26], 1.0, None, ALU.add))
                    link(dve.tensor_copy(ctl[0:1, pairs_at + 1:pairs_at + 2], small[0:1, 25:26]))
                    link(dve.tensor_scalar(small[:, 26:27], part[:], 2.0, float(-BACK), ALU.mult, ALU.add))
                    link(dve.tensor_scalar(of["q"], iota[:, 0:STEPS_AT], small[:, 26:27], None, ALU.add))
                    link(dve.memset(got, 0.0))

                @block.tensor
                def _(pe):
                    pe.wait_ge(s_red, 1)
                    for k in range(KG):
                        for v in range(2):
                            last = pe.transpose(ps[0:sizes[k], k, v * P:(v + 1) * P],
                                                gmm[:, v, k * P:k * P + sizes[k]], ident[:])
                    last.then_inc(s_tr, 1)
                    pe.wait_ge(s_red, 2)
                    for k in range(KG):
                        m = sizes[k]
                        pe.matmul(bank(2, P, NG), spread[0:m, k, 0, :], tri[0:m, k, :], start=(k == 0), stop=(k == KG - 1))
                    for k in range(KG):
                        m = sizes[k]
                        last = pe.matmul(bank(3, P, NG), spread[0:m, k, 1, :], eye[0:m, k, :], start=(k == 0), stop=(k == KG - 1))
                    last.then_inc(s_mm, 1)

            with nc.Block() as block:
                most = (LIST_A if nw == NWA else LIST_M) // P

                @block.vector
                def _(dve):
                    def over_groups(v):
                        return v.unsqueeze(2).broadcast_to([P, STEPS_AT, NG])

                    def over_steps(v):
                        return v.unsqueeze(1).broadcast_to([P, STEPS_AT, NG])

                    chunks = dve.value_load(ctl[0:1, pairs_at + 1:pairs_at + 2], min_val=1, max_val=most)
                    with dve.Fori(0, chunks) as c:
                        n = 0

                        def link(ins):
                            nonlocal n
                            n += 1
                            ins.then_inc(s_l, 1)
                            dve.wait_ge(s_l, OPS * c + n)

                        OPS = 14
                        link(dve.tensor_tensor(hit, over_steps(endv[:, 0, :]), over_groups(of["q"]), ALU.is_le))
                        link(dve.tensor_reduce(of["group"], hit, AX.X, ALU.add))
                        link(dve.tensor_tensor(hit, over_steps(iota[:, 0:NG]), over_groups(of["group"]), ALU.is_equal))
                        link(dve.tensor_tensor(hit, hit, over_steps(endv[:, 1, :]), ALU.mult))
                        link(dve.tensor_reduce(of["window"], hit, AX.X, ALU.add))
                        link(dve.tensor_tensor(of["window"], of["window"], of["q"], ALU.add))
                        link(dve.tensor_scalar(of["group"], of["group"], float(NG - 1), None, ALU.min))
                        dve.tensor_scalar(of["window"], of["window"], float(nw), 0.0, ALU.min, ALU.max)
                        link(dve.tensor_copy(slots_i[:, 0:STEPS_AT], of["group"]))
                        dve.tensor_scalar(slots_i[:, 8:8 + STEPS_AT], slots_i[:, 0:STEPS_AT], ERING - 1, None, ALU.bitwise_and)
                        dve.tensor_scalar(of["row"], of["window"], float(width), None, ALU.mult)
                        link(dve.tensor_scalar(of["ready"], of["group"], 1.0, float(TPG), ALU.add, ALU.mult))
                        link(dve.tensor_scalar(slots_i[:, 0:STEPS_AT], slots_i[:, 0:STEPS_AT], RING - 1, None, ALU.bitwise_and))
                        dve.tensor_copy(of["slot"], slots_i[:, 0:STEPS_AT])
                        link(dve.tensor_copy(of["eslot"], slots_i[:, 8:8 + STEPS_AT]))
                        dve.tensor_scalar(of["slot"], of["slot"], float(TPG * TW), None, ALU.mult)
                        link(dve.tensor_scalar(of["eslot"], of["eslot"], float(GE), None, ALU.mult))
                        for k, entry in enumerate(e for quad in quads for e in quad):
                            if entry:
                                f, d = entry
                                last = dve.tensor_copy(got[:, k:k + 1], of[f][:, d + BACK:d + BACK + 1])
                        link(last)
                        dve.tensor_copy(got_i, got).then_inc(s_rec, 1)
                        link(dve.tensor_scalar(of["q"], of["q"], float(2 * P), None, ALU.add))
                        assert n == OPS
                        dve.wait_ge(s_sent, 16 * c + 16)

                @block.sync
                def _(sp):
                    chunks = sp.value_load(ctl[0:1, pairs_at + 1:pairs_at + 2], min_val=1, max_val=most)
                    with sp.Fori(0, chunks) as c:
                        sp.wait_ge(s_rec, c + 1)
                        sp.dma_start(steps[bass.ds(c * P, P), :], got_i).then_inc(s_sent, 16)
                    sp.wait_ge(s_sent, 16)

        build_steps("m", 7, NWM, ROW_M, QUADS_M, steps_m, ends_m, 0)
        build_steps("a", 5, NWA, ROW_A, QUADS_A, steps_a, ends_a, 2)

        TAIL = E - FULL * CH
        MACRO = FULL // SPAN
        REST = FULL - MACRO * SPAN
        e_in = work[0:DE, 0:2 * SPAN * CH].rearrange("p (b n) -> p b n", b=2)
        relu_u = rows[0:D, :, :, :].rearrange("p r j c -> p (r j c)")[:, 0:4 * CH].rearrange("p (b n) -> p b n", b=4)
        estat = big[0:D, 0:(FULL + 1) * 6].rearrange("p (n s) -> p n s", s=6)
        s_ein = [sem(f"s_ein{b}") for b in range(2)]
        s_u = sem("s_u")
        s_ru = sem("s_ru")
        s_st = sem("s_st")
        s_ew = sem("s_ew")
        s_sq = sem("s_sq")
        with nc.Block() as block:
            @block.sync
            def _(sp):
                for b in range(2):
                    sp.dma_start(e_in[:, b, :], edgeT[:, b * SPAN * CH:(b + 1) * SPAN * CH]).then_inc(s_ein[b], 16)
                with sp.Fori(1, MACRO // 2) as i:
                    for b in range(2):
                        sp.wait_ge(s_u, 2 * SPAN * i - SPAN + SPAN * b)
                        sp.dma_start(e_in[:, b, :],
                                     edgeT[:, bass.ds(i * (2 * SPAN * CH) + b * SPAN * CH, SPAN * CH)]).then_inc(s_ein[b], 16)
                sp.wait_ge(s_u, MACRO * SPAN)
                rest = E - MACRO * SPAN * CH
                sp.dma_start(e_in[:, 0, 0:rest], edgeT[:, MACRO * SPAN * CH:E]).then_inc(s_ein[0], 16)

            @block.tensor
            def _(pe):
                def chunk(b, j, k, n=CH):
                    pe.matmul(bank(k % 4, D, n), wt["We"][:], e_in[:, b, j * CH:j * CH + n],
                              start=True, stop=True).then_inc(s_u, 1)
                for b in range(2):
                    pe.wait_ge(s_ein[b], 16)
                    for j in range(SPAN):
                        k = b * SPAN + j
                        if k >= 4:
                            pe.wait_ge(s_ru, k - 3)
                        chunk(b, j, k)
                with pe.Fori(1, MACRO // 2) as i:
                    for b in range(2):
                        pe.wait_ge(s_ein[b], 16 * i + 16)
                        for j in range(SPAN):
                            pe.wait_ge(s_ru, 2 * SPAN * i + (b * SPAN + j - 3))
                            chunk(b, j, j)
                pe.wait_ge(s_ein[0], 16 * (MACRO // 2) + 16)
                for j in range(REST + 1):
                    k = MACRO * SPAN + j
                    pe.wait_ge(s_ru, k - 3)
                    chunk(0, j, k, CH if j < REST else TAIL)

            @block.scalar
            def _(act):
                def chunk(k, n=CH):
                    nc.scalar.activation(relu_u[:, k % 4, 0:n], bank(k % 4, D, n), ACT.Relu,
                                         bias=cols[:, 3:4]).then_inc(s_ru, 1)
                act.preload_act_table(ACT.Exp)
                for k in range(8):
                    act.wait_ge(s_u, k + 1)
                    if k >= 4:
                        act.wait_ge(s_st, k - 3)
                    chunk(k)
                with act.Fori(1, FULL // 8) as i:
                    for j in range(8):
                        act.wait_ge(s_u, 8 * i + j + 1)
                        act.wait_ge(s_st, 8 * i + (j - 3))
                        chunk(j)
                for k in range(FULL // 8 * 8, FULL + 1):
                    act.wait_ge(s_u, k + 1)
                    act.wait_ge(s_st, k - 3)
                    chunk(k, CH if k < FULL else TAIL)
                act.wait_ge(s_ew, 3)
                nc.scalar.activation(small[0:D, 32:34], small[0:D, 34:36], ACT.Sqrt).then_inc(s_sq, 1)

            @block.vector
            def _(dve):
                with dve.Fori(0, FULL // 4) as i:
                    for j in range(4):
                        dve.wait_ge(s_ru, 4 * i + j + 1)
                        dve.bn_stats(estat[:, bass.ds(4 * i + j, 1), :].rearrange("p n s -> p (n s)"), relu_u[:, j, :]).then_inc(s_st, 1)
                for k in range(FULL // 4 * 4, FULL + 1):
                    dve.wait_ge(s_ru, k + 1)
                    n = CH if k < FULL else TAIL
                    dve.bn_stats(estat[:, k, :], relu_u[:, k % 4, 0:n]).then_inc(s_st, 1)
                dve.wait_ge(s_st, FULL + 1)
                dve.bn_aggr(small[0:D, 36:38], estat.rearrange("p n s -> p (n s)")).then_inc(s_ew, 1)
                dve.wait_ge(s_ew, 1)
                dve.tensor_scalar(small[0:D, 34:36], small[0:D, 36:38], EPS, None, ALU.add).then_inc(s_ew, 2)
                dve.wait_ge(s_sq, 1)
                dve.reciprocal(small[0:D, 38:39], small[0:D, 33:34]).then_inc(s_ew, 1)
                dve.wait_ge(s_ew, 4)
                dve.tensor_tensor(small[0:D, 39:40], small[0:D, 38:39], cols[:, 4:5], ALU.mult).then_inc(s_ew, 1)
                dve.wait_ge(s_ew, 5)
                dve.tensor_scalar(W3s[:], wt["W3"][:], small[0:D, 39:40], None, ALU.mult)
                dve.tensor_tensor(small[0:D, 40:41], small[0:D, 36:37], small[0:D, 39:40], ALU.mult).then_inc(s_ew, 1)
                dve.wait_ge(s_ew, 6)
                dve.tensor_tensor(small[0:D, 41:42], cols[:, 5:6], small[0:D, 40:41], ALU.subtract).then_inc(s_ew, 1)

        nfT = XT[0:D, :]
        big_m = big[:, 0:(NWM + 1) * ROW_M].rearrange("p (w c) -> p w c", c=ROW_M)
        acc_m, base_m, b_rows = big_m[:, :, 0:MW], big_m[:, :, MW], big_m[:, :, MW + 1:ROW_M]
        EDGES_AT = (NWM + 1) * ROW_M
        stage_m = work[:, 0:NT * D].rearrange("p (t c) -> p t c", c=D)
        s_c1 = sem("s_c1")
        s_c2 = sem("s_c2")
        s_t1 = sem("s_t1")
        s_t2 = sem("s_t2")
        s_tab = sem("s_tab")
        s_w = sem("s_w")
        s_wc = sem("s_wc")
        s_n = sem("s_n")
        s_nf = sem("s_nf")
        TB = 4
        NB = -(-NT // TB)
        tiles = [list(range(b * TB, min(NT, b * TB + TB))) for b in range(NB)]
        with nc.Block() as block:
            @block.tensor
            def _(pe):
                pe.matmul(ps[0:1, 7, 0:D], small[0:D, 41:42], wt["W3"][:], start=True, stop=True).then_inc(s_c1, 1)
                for l in range(LAYERS):
                    last = pe.matmul(ps[0:D, 6, l * 2 * H:(l + 1) * 2 * H], wt["WT"][:, l, :], wt["att"][:, l, :],
                                     start=True, stop=True)
                last.then_inc(s_w, 1)
                for b, ts in enumerate(tiles):
                    if b >= 2:
                        pe.wait_ge(s_t2, b - 1)
                    for t in ts:
                        last = pe.matmul(ps[:, b % 2, (t - ts[0]) * D:(t - ts[0] + 1) * D], XT[0:D, t * P:(t + 1) * P],
                                         wt["W1"][:], start=True, stop=True)
                    last.then_inc(s_t1, 1)
                pe.wait_ge(s_c2, 1)
                for b, ts in enumerate(tiles):
                    pe.wait_ge(s_t2, NB + b - 1)
                    for t in ts:
                        o = ps[:, (NB + b) % 2, (t - ts[0]) * D:(t - ts[0] + 1) * D]
                        pe.matmul(o, XT[0:D, t * P:(t + 1) * P], wt["W2"][:], start=True, stop=False)
                        last = pe.matmul(o, ones[0:1, :], rowsb[0:1, 3, :], start=False, stop=True)
                    last.then_inc(s_t1, 1)
                for b in range(NB):
                    n = min(512, NPAD - b * 512)
                    if b >= 4:
                        pe.wait_ge(s_nf, b - 3)
                    pe.matmul(bank(2 + b % 4, D, n), wt["Wn"][:], XT[0:D, b * 512:b * 512 + n],
                              start=True, stop=True).then_inc(s_n, 1)

            @block.vector
            def _(dve):
                dve.wait_ge(s_c1, 1)
                dve.tensor_tensor(rowsb[0:1, 3, :], ps[0:1, 7, 0:D], rowsb[0:1, 0, :], ALU.add).then_inc(s_c2, 1)
                dve.wait_ge(s_w, 1)
                got = ps[0:D, 6, 0:LAYERS * 2 * H].rearrange("p (l k h) -> p l k h", l=LAYERS, k=2)
                dve.tensor_copy(w_all[0:D, :, D + 1:TW], got[:, :, 0, :])
                dve.tensor_copy(z_all[:, :, WA - 1:ZW:WA], got[:, :, 1, :])
                dve.memset(b_rows[:, NT, :], 0.0)
                for k in range(2):
                    for b, ts in enumerate(tiles):
                        dve.wait_ge(s_t1, k * NB + b + 1)
                        to = stage_m if k == 0 else b_rows
                        dve.tensor_copy(to[:, ts[0]:ts[-1] + 1, :],
                                        ps[:, (k * NB + b) % 2, 0:len(ts) * D].rearrange("p (t c) -> p t c", c=D)).then_inc(s_t2, 1)
                dve.memset(acc_m, 0.0)
                dve.tensor_scalar(base_m, iota[:, 0:NWM + 1], float(WM), None, ALU.mult)

            @block.sync
            def _(sp):
                sp.wait_ge(s_t2, NB)
                sp.dma_start(table_m.rearrange("(t p) c -> p t c", p=P), stage_m).then_inc(s_tab, 16)
                sp.wait_ge(s_tab, 16)

            @block.scalar
            def _(act):
                for b in range(NB):
                    n = min(512, NPAD - b * 512)
                    act.wait_ge(s_n, b + 1)
                    nc.scalar.activation(nfT[:, b * 512:b * 512 + n], bank(2 + b % 4, D, n), ACT.Relu,
                                         bias=cols[:, 0:1]).then_inc(s_nf, 1)

        def edge_block(steps, ends, pairs_at, quads, nw, table, width, with_edges, emit, passes):
            s_idx = [emit.sems[f"idx{k}"] for k in range(RING)]
            s_gat = [emit.sems[f"gat{k}"] for k in range(RING)]
            s_edge = [emit.sems[f"edge{k}"] for k in range(RING)]
            landed, begun, done = emit.sems["landed"], emit.sems["begun"], emit.sems["done"]
            src_v = src.rearrange("(g p j) -> g p j", p=P, j=TPG)

            with nc.Block() as block:
                @block.sync
                def _(sp):
                    def load_indices(g, k):
                        sp.dma_start(idx[:, k, :], src_v[g] if isinstance(g, int) else
                                     src_v[bass.ds(g, 1)].rearrange("g p j -> p (g j)")).then_inc(s_idx[k], 16)

                    def load_edges(g, k):
                        sp.dma_start(big[0:DE, EDGES_AT + k * GE:EDGES_AT + (k + 1) * GE], edgeT[:, bass.ds(g * GE, GE)]).then_inc(s_edge[k], 16)

                    def hand_over(k, turn, ek, eturn):
                        sp.wait_ge(s_gat[k], before[len(range(k, NG, RING))] + turn * (16 * TPG) + 16 * TPG)
                        if with_edges:
                            sp.wait_ge(s_edge[ek], eturn * 16 + 16)
                        sp.sem_inc(landed, TPG)

                    def refill(g, k, ek, more):
                        end = sp.value_load(ends[0:1, bass.ds(g - LAG, 1)], min_val=1, max_val=NG * (nw + 1))
                        sp.wait_ge(done, end)
                        if more:
                            load_indices(g - LAG + RING, k)
                        if with_edges:
                            load_edges(g - LAG + ERING, ek)

                    before = {n: passes * (16 * TPG * n) if isinstance(passes, int) else sp.snap(passes * (16 * TPG * n))
                              for n in {len(range(k, NG, RING)) for k in range(RING)}}
                    for g in range(RING):
                        load_indices(g, g)
                    if with_edges:
                        for g in range(ERING):
                            load_edges(g, g)
                    for g in range(LAG):
                        hand_over(g, 0, g, 0)
                    LOOPS = (NG - RING) // RING
                    with sp.Fori(0, LOOPS) as i:
                        for u in range(RING):
                            k = LAG + u
                            hand_over(k % RING, i + k // RING, k % ERING, i * (RING // ERING) + k // ERING)
                            refill(i * RING + k, u, u % ERING, True)
                    for g in range(LAG + LOOPS * RING, NG):
                        hand_over(g % RING, g // RING, g % ERING, g // ERING)
                        if g - LAG + RING < NG or with_edges and g - LAG + ERING < NG:
                            refill(g, (g - LAG) % RING, (g - LAG) % ERING, g - LAG + RING < NG)

                @block.gpsimd
                def _(pool):
                    def gather(k, turn):
                        pool.wait_ge(s_idx[k], turn * 16 + 16)
                        pool.sem_inc(begun, 1)
                        for j in range(TPG):
                            pool.indirect_dma_start(rows[:, k, j, 0:width], None, table,
                                                    bass.IndirectOffsetOnAxis(ap=idx[:, k, j:j + 1], axis=0)).then_inc(s_gat[k], 16)
                    with pool.Fori(0, NG // RING) as i:
                        for k in range(RING):
                            gather(k, i)
                    for k in range(NG % RING):
                        gather(k, NG // RING)

                def take_pairs(eng, wanted, step):
                    most = (PAIRS_A if nw == NWA else PAIRS_M) - 2
                    pairs = SURE + eng.value_load(ctl[0:1, pairs_at:pairs_at + 1], min_val=NG // 2 - SURE, max_val=most - SURE)

                    bounds = dict(row=(0, nw * (ROW_A if nw == NWA else ROW_M)), ready=(TPG, NG * TPG),
                                  slot=(0, (RING - 1) * TPG * TW), eslot=(0, (ERING - 1) * GE))

                    def pair(i, parities, live):
                        told = {}
                        for k in wanted:
                            _, values = nc.values_load_multi_w_load_instructions(
                                steps[bass.ds(i, 1), 4 * k:4 * k + 4], engines=[eng.engine], min_val=0, max_val=TOP)
                            told |= {e: nc.s_assert_within(v, *bounds[e[0]], skip_runtime_bounds_check_because=
                                                           "the list is made of steps within these bounds")
                                     for e, v in zip(quads[k], values) if e}
                        for par in parities:
                            step(2 * i + par, par, lambda lag: live(par, lag), lambda f, lag: told[f, par - lag])

                    pair(0, (0, 1), lambda par, lag: lag <= par)
                    pair(1, (0, 1), lambda par, lag: lag <= 2 + par)
                    with eng.Fori(2, pairs) as i:
                        pair(i, (0, 1), lambda par, lag: True)
                    pair(pairs, (0, 1), lambda par, lag: lag > par)
                    if LAG > 2:
                        pair(pairs + 1, (0,), lambda par, lag: lag > 2)

                @block.vector
                def _(dve):
                    take_pairs(dve, emit.vector_quads, emit.vector(dve))

                @block.scalar
                def _(act):
                    act.preload_act_table(ACT.Exp)
                    take_pairs(act, emit.scalar_quads, emit.scalar(act))

                @block.tensor
                def _(pe):
                    take_pairs(pe, emit.tensor_quads, emit.tensor(pe))

        shared = {f"{n}{k}": sem(f"{n}{k}") for n in ("idx", "gat", "edge") for k in range(RING)}
        shared |= {n: sem(n) for n in ("landed", "begun", "done")}
        cleared = [v for n, v in shared.items() if not n.startswith("gat")]
        step_sems = {n: sem(n) for n in (
            "eq_ready", "eqt_ready", "eqts_ready", "u_ready", "ut_ready", "pre_ready", "v_ready", "relu_done",
            "rr_ready", "s_ready")}

        eq = work[:, 0:2 * TPG * P].rearrange("p (s j n) -> p s j n", s=2, j=TPG)
        eqT = work[:, 2048:2048 + TPG * P].rearrange("p (j n) -> p j n", j=TPG)
        uT = work[0:D, 3072:3072 + GE]
        vsum = work[:, 4096:4096 + TPG * D].rearrange("p (j c) -> p j c", j=TPG)
        rr = work[:, 5120:5120 + TPG * MW].rearrange("p (j c) -> p j c", j=TPG)
        
        def rows_of(slot):
            return rows[:].rearrange("p r j c -> p (r j c)")[:, bass.ds(slot, TPG * TW)].rearrange("p (j c) -> p j c", c=TW)

        class Message:
            sems = shared
            vector_quads, scalar_quads, tensor_quads = (0, 1), (), (0, 2)

            @staticmethod
            def vector(dve):
                s = step_sems

                def accumulate(k, par, at):
                    dve.wait_ge(s["s_ready"], k + 1)
                    if not (isinstance(k, int) and k == 0):
                        dve.wait_ge(shared["done"], k)
                    a = big[:, bass.ds(at("row", 2), MW)]
                    dve.tensor_tensor(a, a, ps[:, 6 + par, 0:MW], ALU.add).then_inc(shared["done"], 1)

                def match(q, par, at):
                    dve.wait_ge(shared["landed"], at("ready", 0))
                    d = dstf[:, bass.ds(at("ready", 0), TPG)].unsqueeze(2).broadcast_to([P, TPG, WM])
                    dve.scalar_tensor_tensor(eq[:, par], d, big[:, bass.ds(at("row", 0) + MW, 1)],
                                             iota[:, 0:WM].unsqueeze(1).broadcast_to([P, TPG, WM]),
                                             ALU.subtract, ALU.is_equal).then_inc(s["eq_ready"], 1)

                def add_source(k, par, at):
                    dve.wait_ge(s["pre_ready"], k + 1)
                    if not (isinstance(k, int) and k == 0):
                        dve.wait_ge(s["rr_ready"], k)
                    for half in range(2):
                        j0 = half * TPG // 2
                        ins = dve.tensor_tensor(
                            vsum[:, j0:j0 + TPG // 2, :],
                            ps[:, 4 + half, 0:TPG // 2 * D].rearrange("p (j c) -> p j c", c=D),
                            rows_of(at("slot", 1))[:, j0:j0 + TPG // 2, 0:D], ALU.add)
                    ins.then_inc(s["v_ready"], 1)
                def step(q, par, live, at):
                    if live(2):
                        accumulate(q - 2, (par - 2) % 2, at)
                    if live(0):
                        match(q, par, at)
                    if live(1):
                        add_source(q - 1, (par - 1) % 2, at)
                return step

            @staticmethod
            def scalar(act):
                s = step_sems

                def copy_match(q, par, at):
                    act.wait_ge(s["eqt_ready"], q + 1)
                    if not (isinstance(q, int) and q == 0):
                        act.wait_ge(s["pre_ready"], q)
                    nc.scalar.activation(eqT, ps[:, 0:2, :].rearrange("p b (j n) -> p (b j) n", n=P), ACT.Copy).then_inc(s["eqts_ready"], 1)

                def edge_relu(q, par, at):
                    act.wait_ge(s["u_ready"], q + 1)
                    nc.scalar.activation(uT, ps[0:D, 2:4, :].rearrange("p b n -> p (b n)"), ACT.Relu, bias=cols[:, 3:4]).then_inc(s["ut_ready"], 1)

                def message_relu(k, par, at):
                    act.wait_ge(s["v_ready"], k + 1)
                    if not (isinstance(k, int) and k == 0):
                        act.wait_ge(s["s_ready"], k)
                    nc.scalar.activation(rr[:, :, 0:D], vsum, ACT.Relu).then_inc(s["relu_done"], 1)
                    act.wait_ge(s["relu_done"], k + 1)
                    nc.scalar.activation(rr[:, :, D:2 * D], rr[:, :, 0:D], ACT.Square).then_inc(s["rr_ready"], 1)
                def step(q, par, live, at):
                    if live(0):
                        copy_match(q, par, at)
                    if live(0):
                        edge_relu(q, par, at)
                    if live(1):
                        message_relu(q - 1, (par - 1) % 2, at)
                return step

            @staticmethod
            def tensor(pe):
                s = step_sems

                def turn_match(q, par, at):
                    pe.wait_ge(s["eq_ready"], q + 1)
                    if not (isinstance(q, int) and q == 0):
                        pe.wait_ge(s["eqts_ready"], q)
                    for j in range(TPG):
                        last = pe.transpose(ps[:, j // 4, (j % 4) * P:(j % 4 + 1) * P], eq[:, par, j, :], ident[:])
                    last.then_inc(s["eqt_ready"], 1)

                def edge_product(q, par, at):
                    pe.wait_ge(shared["landed"], at("ready", 0))
                    if not (isinstance(q, int) and q == 0):
                        pe.wait_ge(s["ut_ready"], q)
                    for half in range(2):
                        last = pe.matmul(bank(2 + half, D, 512), wt["We"][:],
                                         big[0:DE, bass.ds(at("eslot", 0) + (EDGES_AT + half * 512), 512)],
                                         start=True, stop=True)
                    last.then_inc(s["u_ready"], 1)

                def message_product(k, par, at):
                    pe.wait_ge(s["eqts_ready"], k + 1)
                    pe.wait_ge(s["ut_ready"], k + 1)
                    if not (isinstance(k, int) and k == 0):
                        pe.wait_ge(s["v_ready"], k)
                    ut = uT.rearrange("p (e j) -> p j e", j=TPG)
                    b_w = big[:, bass.ds(at("row", 1) + (MW + 1), D)]
                    for j in range(TPG):
                        o = ps[:, 4 + j // 4, (j % 4) * D:(j % 4 + 1) * D]
                        pe.matmul(o, ut[:, j, :], W3s[:], start=True, stop=False)
                        last = pe.matmul(o, eqT[:, j, :], b_w, start=False, stop=True)
                    last.then_inc(s["pre_ready"], 1)

                def node_sums(k, par, at):
                    pe.wait_ge(s["rr_ready"], k + 1)
                    if not (isinstance(k, int) and k < 2):
                        pe.wait_ge(shared["done"], k - 1)
                    for j in range(TPG):
                        last = pe.matmul(ps[:, 6 + par, 0:MW], eq[:, par, j, :], rr[:, j, :], start=(j == 0), stop=(j == TPG - 1))
                    last.then_inc(s["s_ready"], 1)
                def step(q, par, live, at):
                    if live(0):
                        edge_product(q, par, at)
                    if live(2):
                        node_sums(q - 2, (par - 2) % 2, at)
                    if live(0):
                        turn_match(q, par, at)
                    if live(1):
                        message_product(q - 1, (par - 1) % 2, at)
                return step

        with nc.Block() as block:
            @block.vector
            def _(dve):
                dve.memset(rr[:, :, 2 * D:MW], 1.0)
        edge_block(steps_m, ends_m, 0, QUADS_M, NWM, table_m, D, True, Message, 0)

        s_pe3 = sem("s_pe3")
        s_asked = sem("s_asked")
        s_rooted = sem("s_rooted")
        s_xt = sem("s_xt")
        s_d3 = sem("s_d3")
        s_v3 = sem("s_v3")
        s_add = sem("s_add")

        def layer_norm(dve, link, asked, rooted, value):
            for t in range(NT):
                last = dve.bn_stats(lnst[:, t, :], xn[:, t, :])
            link(last)
            for t in range(NT):
                last = dve.bn_aggr(lnmv[:, t, :], lnst[:, t, :])
            link(last)
            dve.tensor_scalar(lnr[:], lnmv[:, :, 1], EPS, None, ALU.add).then_inc(asked, 1)
            dve.wait_ge(rooted, value)
            link(dve.reciprocal(lnr[:], lnr[:]))
            for t in range(NT):
                last = dve.tensor_scalar(xn[:, t, :], xn[:, t, :], lnmv[:, t, 0:1], lnr[:, t:t + 1], ALU.subtract, ALU.mult)
            return last

        with nc.Block() as block:
            @block.tensor
            def _(pe):
                pe.matmul(ps[:, 1, 0:2 * D], ones[0:1, :], rowsb[0:1, 1:3, :].rearrange("p k c -> p (k c)"),
                          start=True, stop=True)
                pe.wait_ge(s_d3, 1)
                for t in range(NT):
                    last = pe.matmul(ps[:, 0, 0:2 * D], ones[:], big_m[:, t, 0:2 * D], start=(t == 0), stop=(t == NT - 1))
                last.then_inc(s_pe3, 1)
                pe.wait_ge(s_v3, 1)
                for b, ts in enumerate(tiles):
                    if b >= 2:
                        pe.wait_ge(s_add, b - 1)
                    for t in ts:
                        last = pe.transpose(ps[:, 2 + b % 2, (t - ts[0]) * D:(t - ts[0] + 1) * D],
                                            nfT[:, t * P:(t + 1) * P], ident[0:D, 0:D])
                    last.then_inc(s_pe3, 1)
                pe.wait_ge(s_v3, 2)
                for b, ts in enumerate(tiles):
                    if b >= 2:
                        pe.wait_ge(s_xt, b - 1)
                    for t in ts:
                        last = pe.transpose(ps[0:D, 4 + b % 2, (t - ts[0]) * P:(t - ts[0] + 1) * P], xn[:, t, :], ident[:])
                    last.then_inc(s_pe3, 1)

            @block.scalar
            def _(act):
                act.wait_ge(s_asked, 1)
                nc.scalar.activation(rowsb[:, 4, :], rowsb[:, 4, :], ACT.Sqrt).then_inc(s_rooted, 1)
                act.wait_ge(s_asked, 2)
                nc.scalar.activation(small[0:D, 44:46], small[0:D, 42:44], ACT.Sqrt).then_inc(s_rooted, 1)
                act.wait_ge(s_asked, 3)
                nc.scalar.activation(lnr[:], lnr[:], ACT.Sqrt).then_inc(s_rooted, 1)
                for b, ts in enumerate(tiles):
                    act.wait_ge(s_pe3, 1 + NB + b + 1)
                    nc.scalar.activation(XT[0:D, ts[0] * P:(ts[-1] + 1) * P], ps[0:D, 4 + b % 2, 0:len(ts) * P],
                                         ACT.Copy).then_inc(s_xt, 1)

            @block.vector
            def _(dve):
                n = 1

                def link(ins):
                    nonlocal n
                    n += 1
                    ins.then_inc(s_d3, 1)
                    dve.wait_ge(s_d3, n)

                dve.tensor_scalar(acc_m[:, NT - 1, :], acc_m[:, NT - 1, :], rowmask[:, 0:1], None, ALU.mult).then_inc(s_d3, 1)
                dve.wait_ge(s_d3, 1)
                for b in range(NB):
                    m = min(512, N - b * 512)
                    last = dve.bn_stats(lnst[0:D, b, :], nfT[:, b * 512:b * 512 + m])
                link(last)
                link(dve.bn_aggr(small[0:D, 42:44], lnst[0:D, 0:NB, :].rearrange("p n s -> p (n s)")))
                link(dve.tensor_copy(small[0:D, 46:47], small[0:D, 42:43]))
                dve.wait_ge(s_pe3, 1)
                link(dve.tensor_copy(rowsb[:, 6:8, :], ps[:, 1, 0:2 * D].rearrange("p (k c) -> p k c", k=2)))
                link(dve.tensor_scalar(rowsb[:, 3:5, :], ps[:, 0, 0:2 * D].rearrange("p (k c) -> p k c", k=2), 1.0 / E, None, ALU.mult))
                link(dve.tensor_tensor(rowsb[:, 5, :], rowsb[:, 3, :], rowsb[:, 3, :], ALU.mult))
                link(dve.tensor_tensor(rowsb[:, 4, :], rowsb[:, 4, :], rowsb[:, 5, :], ALU.subtract))
                dve.tensor_scalar(rowsb[:, 4, :], rowsb[:, 4, :], 0.0, EPS, ALU.max, ALU.add).then_inc(s_asked, 1)
                dve.wait_ge(s_rooted, 1)
                link(dve.reciprocal(rowsb[:, 4, :], rowsb[:, 4, :]))
                link(dve.tensor_tensor(rowsb[:, 4, :], rowsb[:, 4, :], rowsb[:, 6, :], ALU.mult))
                link(dve.tensor_tensor(rowsb[:, 5, :], rowsb[:, 3, :], rowsb[:, 4, :], ALU.mult))
                link(dve.tensor_tensor(rowsb[:, 5, :], rowsb[:, 7, :], rowsb[:, 5, :], ALU.subtract))
                dve.tensor_scalar(small[0:D, 42:44], small[0:D, 42:44], EPS, None, ALU.add).then_inc(s_asked, 1)
                dve.wait_ge(s_rooted, 2)
                link(dve.reciprocal(small[0:D, 44:45], small[0:D, 45:46]))
                link(dve.tensor_tensor(small[0:D, 44:45], small[0:D, 44:45], cols[:, 1:2], ALU.mult))
                link(dve.tensor_tensor(small[0:D, 47:48], small[0:D, 46:47], small[0:D, 44:45], ALU.mult))
                link(dve.tensor_tensor(small[0:D, 47:48], cols[:, 2:3], small[0:D, 47:48], ALU.subtract))
                dve.tensor_scalar(nfT, nfT, small[0:D, 44:45], small[0:D, 47:48], ALU.mult, ALU.add).then_inc(s_v3, 1)
                sums, spare, degree = acc_m[:, 0:NT, 0:D], acc_m[:, 0:NT, D:2 * D], acc_m[:, 0:NT, 2 * D:MW]
                dve.tensor_tensor(sums, sums, rowsb[:, 4, :].unsqueeze(1).broadcast_to([P, NT, D]), ALU.mult)
                link(dve.tensor_tensor(spare, degree.broadcast_to([P, NT, D]), rowsb[:, 5, :].unsqueeze(1).broadcast_to([P, NT, D]), ALU.mult))
                link(dve.tensor_tensor(sums, sums, spare, ALU.add))
                link(dve.tensor_tensor(xn[:], xn[:], sums, ALU.add))
                for b, ts in enumerate(tiles):
                    dve.wait_ge(s_pe3, 1 + b + 1)
                    a = xn[:, ts[0]:ts[-1] + 1, :]
                    last = dve.tensor_tensor(a, a, ps[:, 2 + b % 2, 0:len(ts) * D].rearrange("p (t c) -> p t c", c=D), ALU.add)
                    last.then_inc(s_add, 1)
                dve.wait_ge(s_add, NB)
                layer_norm(dve, link, s_asked, s_rooted, 3).then_inc(s_v3, 1)

        NEGMAX, BASE, LOGIT = D + 1, D + 2, D + 3
        acc = big[:].rearrange("p (w c) -> p w c", c=ROW_A)
        stage = work[:, 0:NT * TW].rearrange("p (t c) -> p t c", c=TW)
        rden = sb("rden", [P, NWA])
        ne = work[:, 7168:7168 + TPG * WA].rearrange("p (j n) -> p j n", j=TPG)
        masked = work[:, 0:2048].rearrange("p (s j h n) -> p s j h n", s=2, j=TPG, h=H)
        positive = work[:, 2048:3072]
        logit = work[:, 7424:9472].rearrange("p (s n) -> p s n", s=2)
        prob = work[:, 3072:5120].rearrange("p (s j e) -> p s j e", s=2, j=TPG)
        probT = work[:, 5120:7168].rearrange("p (s j e) -> p s j e", s=2, j=TPG)
        locmax, neg, keep = (small[:, 48 + 2 * k:50 + 2 * k] for k in range(3))
        a_sems = {n: sem(n) for n in (
            "ne_ready", "a_ready", "t_ready", "positive_ready", "max_ready", "neg_ready", "keep_ready",
            "saved", "p_ready", "pt_ready", "pts_ready", "o_ready", "paced", "turned")}

        class Attention:
            sems = shared
            vector_quads, scalar_quads, tensor_quads = (0, 1, 2), (0,), (2,)

            @staticmethod
            def vector(dve):
                s = a_sems

                def accumulate(k, par, at):
                    dve.wait_ge(s["o_ready"], k + 1)
                    if not (isinstance(k, int) and k == 0):
                        dve.wait_ge(shared["done"], k)
                    a = big[:, bass.ds(at("row", 3), D + 1)]
                    dve.scalar_tensor_tensor(a, a, keep[:, par:par + 1], ps[:, 6 + par, 0:D + 1], ALU.mult, ALU.add).then_inc(shared["done"], 1)

                def maximum(k, par, at):
                    dve.wait_ge(s["positive_ready"], k + 1)
                    if not (isinstance(k, int) and k < 2):
                        dve.wait_ge(s["p_ready"], k - 1)
                    dve.sem_inc(s["turned"], 1)
                    dve.tensor_tensor_reduce(out=logit[:, par], in0=positive, in1=ps[:, 2 * par:2 * par + 2, :].rearrange("p b n -> p (b n)"),
                                             scale=SLOPE, scalar=3 * MASKED, op0=ALU.add, op1=ALU.max,
                                             accum_out=locmax[:, par:par + 1]).then_inc(s["max_ready"], 1)

                def mask(q, par, at):
                    dve.wait_ge(shared["landed"], at("ready", 0))
                    d = dstf[:, bass.ds(at("ready", 0), TPG)].unsqueeze(2).broadcast_to([P, TPG, WA])
                    if not (isinstance(q, int) and q == 0):
                        dve.wait_ge(s["a_ready"], q)
                    dve.scalar_tensor_tensor(ne, d, big[:, bass.ds(at("row", 0) + BASE, 1)],
                                             iota[:, 0:WA].unsqueeze(1).broadcast_to([P, TPG, WA]),
                                             ALU.subtract, ALU.not_equal).then_inc(s["ne_ready"], 1)
                    dve.wait_ge(s["ne_ready"], q + 1)
                    for h in range(H):
                        source = rows_of(at("slot", 0))[:, :, D + 1 + h].unsqueeze(2).broadcast_to([P, TPG, WA])
                        last = dve.scalar_tensor_tensor(masked[:, par, :, h, :], ne, MASKED, source, ALU.mult, ALU.add)
                    last.then_inc(s["a_ready"], 1)

                def running(k, par, at):
                    dve.wait_ge(s["max_ready"], k + 1)
                    if not (isinstance(k, int) and k == 0):
                        dve.wait_ge(s["saved"], k)
                    dve.scalar_tensor_tensor(neg[:, par:par + 1], locmax[:, par:par + 1], -1.0, big[:, bass.ds(at("row", 1) + NEGMAX, 1)],
                                             ALU.mult, ALU.min).then_inc(s["neg_ready"], 1)
                def step(q, par, live, at):
                    if live(3):
                        accumulate(q - 3, (par - 3) % 2, at)
                    if live(0):
                        mask(q, par, at)
                    if live(1):
                        maximum(q - 1, (par - 1) % 2, at)
                    if live(1):
                        running(q - 1, (par - 1) % 2, at)
                return step

            @staticmethod
            def scalar(act):
                s = a_sems

                def positives(k, par, at):
                    act.wait_ge(s["t_ready"], k + 1)
                    if not (isinstance(k, int) and k == 0):
                        act.wait_ge(s["max_ready"], k)
                    act.sem_inc(s["paced"], 1)
                    nc.scalar.activation(positive, ps[:, 2 * par:2 * par + 2, :].rearrange("p b n -> p (b n)"), ACT.Relu,
                                         bias=big[:, bass.ds(at("row", 1) + LOGIT, 1)], scale=GAIN).then_inc(s["positive_ready"], 1)

                def copy_probs(k, par, at):
                    act.wait_ge(s["pt_ready"], k + 1)
                    if not (isinstance(k, int) and k < 2):
                        act.wait_ge(s["o_ready"], k - 1)
                    nc.scalar.activation(probT[:, par], ps[:, 4:6, :].rearrange("p b (j n) -> p (b j) n", n=P), ACT.Copy).then_inc(s["pts_ready"], 1)

                def exponentials(k, par, at):
                    act.wait_ge(s["neg_ready"], k + 1)
                    if not (isinstance(k, int) and k < 2):
                        act.wait_ge(shared["done"], k - 1)
                    if not (isinstance(k, int) and k == 0):
                        act.wait_ge(s["saved"], k)
                    negmax = big[:, bass.ds(at("row", 1) + NEGMAX, 1)]
                    act.sem_inc(s["paced"], 1)
                    nc.scalar.activation(keep[:, par:par + 1], negmax, ACT.Exp, bias=neg[:, par:par + 1],
                                         scale=-1.0).then_inc(s["keep_ready"], 1)
                    nc.scalar.activation(prob[:, par].rearrange("p j e -> p (j e)"), logit[:, par], ACT.Exp, bias=neg[:, par:par + 1]).then_inc(s["p_ready"], 1)
                    act.wait_ge(s["keep_ready"], k + 1)
                    act.sem_inc(s["turned"], 1)
                    nc.scalar.activation(negmax, neg[:, par:par + 1], ACT.Copy).then_inc(s["saved"], 1)
                def step(q, par, live, at):
                    if live(1):
                        positives(q - 1, (par - 1) % 2, at)
                    if live(2):
                        copy_probs(q - 2, (par - 2) % 2, at)
                    if live(1):
                        exponentials(q - 1, (par - 1) % 2, at)
                return step

            @staticmethod
            def tensor(pe):
                s = a_sems

                def turn_probs(k, par, at):
                    pe.wait_ge(s["p_ready"], k + 1)
                    if not (isinstance(k, int) and k == 0):
                        pe.wait_ge(s["pts_ready"], k)
                    for j in range(TPG):
                        last = pe.transpose(ps[:, 4 + j // 4, (j % 4) * P:(j % 4 + 1) * P], prob[:, par, j, :], ident[:])
                    last.then_inc(s["pt_ready"], 1)

                def turn_mask(q, par, at):
                    pe.wait_ge(s["a_ready"], q + 1)
                    if not (isinstance(q, int) and q < 2):
                        pe.wait_ge(s["max_ready"], q - 1)
                    for j in range(TPG):
                        last = pe.transpose(ps[:, 2 * par + j // 4, (j % 4) * P:(j % 4 + 1) * P],
                                            masked[:, par, j].rearrange("p h n -> p (h n)"), ident[:])
                    last.then_inc(s["t_ready"], 1)

                def weighted_sums(k, par, at):
                    pe.wait_ge(s["pts_ready"], k + 1)
                    if not (isinstance(k, int) and k < 2):
                        pe.wait_ge(shared["done"], k - 1)
                    for j in range(TPG):
                        last = pe.matmul(ps[:, 6 + par, 0:D + 1], probT[:, par, j, :],
                                         rows_of(at("slot", 2))[:, j, 0:D + 1],
                                         start=(j == 0), stop=(j == TPG - 1))
                    last.then_inc(s["o_ready"], 1)
                def step(q, par, live, at):
                    if live(2):
                        turn_probs(q - 2, (par - 2) % 2, at)
                    if live(0):
                        turn_mask(q, par, at)
                    if live(2):
                        weighted_sums(q - 2, (par - 2) % 2, at)
                return step

        s_wl = sem("s_wl")
        s_zero = sem("s_zero")
        s_lt = sem("s_lt")
        s_lc = sem("s_lc")
        s_ad = sem("s_ad")
        s_ta = sem("s_ta")
        s_r = sem("s_r")
        s_m1 = sem("s_m1")
        s_m2 = sem("s_m2")
        s_fo = sem("s_fo")
        s_x = sem("s_x")
        WPB = 512 // WA
        WB = -(-NWA // WPB)
        windows = [(b * WPB, min(NWA, b * WPB + WPB)) for b in range(WB)]
        half = [(4 * b, min(NT, 4 * b + 4)) for b in range(NB)]

        with nc.Block() as block:
            @block.gpsimd
            def _(pool):
                for v in cleared:
                    pool.sem_clear(v)

        with nc.Fori(0, LAYERS) as l:
            with nc.Block() as block:
                @block.vector
                def _(dve):
                    dve.tensor_copy(w_l[:], w_all[:, bass.ds(l, 1), :].rearrange("p l c -> p (l c)"))
                    dve.tensor_copy(z_l[:], z_all[:, bass.ds(l, 1), :].rearrange("p l c -> p (l c)"))
                    dve.tensor_copy(bias_l[:], bias_all[:, bass.ds(l, 1)]).then_inc(s_wl, 1)
                    
                    for b, ts in enumerate(tiles):
                        if b % 2 == 0:
                            dve.wait_ge(s_lt, b + 1)
                            dve.tensor_copy(stage[:, ts[0]:ts[-1] + 1, :],
                                            ps[:, b % 4, 0:len(ts) * TW].rearrange("p (t c) -> p t c", c=TW)).then_inc(s_lc, 1)
                    dve.wait_ge(s_ad, 1)
                    dve.wait_ge(s_zero, 1)
                    dve.tensor_scalar(acc[:, 0:NWA, LOGIT], ps[:, 4, 0:NWA], GAIN, None, ALU.mult)
                    dve.memset(acc[:, :, NEGMAX], FLOOR)

                @block.gpsimd
                def _(pool):
                    pool.memset(big[:], 0.0).then_inc(s_zero, 1)
                    pool.wait_ge(s_zero, 1)
                    pool.iota(acc[:, :, BASE], [[WA, NWA + 1]], base=0, channel_multiplier=0,
                              allow_small_or_imprecise_dtypes=True)

                @block.tensor
                def _(pe):
                    pe.wait_ge(s_wl, 1)
                    for b, ts in enumerate(tiles):
                        if b >= 4:
                            pe.wait_ge(s_lc if b % 2 == 0 else s_m1, (b - 4) // 2 + 1)
                        for t in ts:
                            last = pe.matmul(ps[:, b % 4, (t - ts[0]) * TW:(t - ts[0] + 1) * TW], XT[:, t * P:(t + 1) * P], w_l[:],
                                             start=True, stop=True)
                        last.then_inc(s_lt, 1)
                    xv = XT[0:D, :].rearrange("p (w n) -> p n w", n=WA)
                    for n in range(WA):
                        last = pe.matmul(ps[:, 4, 0:NWA], z_l[:, WA - 1 - n:WA - 1 - n + P], xv[:, n, :],
                                         start=(n == 0), stop=(n == WA - 1))
                    last.then_inc(s_ad, 1)

                @block.scalar
                def _(act):
                    for b, ts in enumerate(tiles):
                        if b % 2 == 1:
                            act.wait_ge(s_lt, b + 1)
                            nc.scalar.activation(stage[:, ts[0]:ts[-1] + 1, :],
                                                 ps[:, b % 4, 0:len(ts) * TW].rearrange("p (t c) -> p t c", c=TW), ACT.Copy).then_inc(s_m1, 1)

                @block.sync
                def _(sp):
                    sp.wait_ge(s_lc, (NB + 1) // 2)
                    sp.wait_ge(s_m1, NB // 2)
                    sp.dma_start(table_a.rearrange("(t p) c -> p t c", p=P), stage).then_inc(s_ta, 16)
                    sp.wait_ge(s_ta, 16)

            edge_block(steps_a, ends_a, 2, QUADS_A, NWA, table_a, TW, False, Attention, l + 1)

            with nc.Block() as block:
                @block.vector
                def _(dve):
                    dve.tensor_scalar(rden[:], acc[:, 0:NWA, D], 1e-16, None, ALU.add).then_inc(s_r, 1)
                    dve.wait_ge(s_r, 1)
                    dve.reciprocal(rden[:], rden[:]).then_inc(s_r, 1)
                    dve.wait_ge(s_r, 2)
                    for b, (w0, w1) in enumerate(windows):
                        a = acc[:, w0:w1, 0:D]
                        dve.tensor_tensor(a, a, rden[:, w0:w1].unsqueeze(2).broadcast_to([P, w1 - w0, D]), ALU.mult).then_inc(s_r, 1)
                        dve.wait_ge(s_r, 3 + b)
                        dve.tensor_tensor(a, a, headmask[:].unsqueeze(1).broadcast_to([P, w1 - w0, D]), ALU.mult).then_inc(s_m2, 1)

                @block.tensor
                def _(pe):
                    for b, (w0, w1) in enumerate(windows):
                        pe.wait_ge(s_m2, b + 1)
                        if b >= 4:
                            pe.wait_ge(s_x, b - 3)
                        for w in range(w0, w1):
                            last = pe.matmul(ps[0:D, b % 4, (w - w0) * WA:(w - w0 + 1) * WA], acc[:, w, 0:D], fold[:], start=True, stop=True)
                        last.then_inc(s_fo, 1)

                @block.scalar
                def _(act):
                    for b, (w0, w1) in enumerate(windows):
                        act.wait_ge(s_fo, b + 1)
                        nc.scalar.activation(XT[0:D, w0 * WA:w1 * WA], ps[0:D, b % 4, 0:(w1 - w0) * WA], ACT.Relu,
                                             bias=bias_l[:, 0:1]).then_inc(s_x, 1)

            with nc.Block() as block:
                @block.gpsimd
                def _(pool):
                    for v in (*cleared, *a_sems.values(), s_zero, s_wl, s_lt, s_lc, s_ad, s_ta, s_r, s_m1, s_m2, s_fo, s_x):
                        pool.sem_clear(v)

        s_back = sem("s_back")
        s_res = sem("s_res")
        s_ask5 = sem("s_ask5")
        s_root5 = sem("s_root5")
        s_d5 = sem("s_d5")
        s_fin = sem("s_fin")
        s_out = sem("s_out")
        with nc.Block() as block:
            @block.tensor
            def _(pe):
                for b, ts in enumerate(tiles):
                    if b >= 4:
                        pe.wait_ge(s_res, b - 3)
                    for t in ts:
                        last = pe.transpose(ps[:, b % 4, (t - ts[0]) * D:(t - ts[0] + 1) * D], XT[0:D, t * P:(t + 1) * P], ident[0:D, 0:D])
                    last.then_inc(s_back, 1)

            @block.scalar
            def _(act):
                act.wait_ge(s_ask5, 1)
                nc.scalar.activation(lnr[:], lnr[:], ACT.Sqrt).then_inc(s_root5, 1)

            @block.vector
            def _(dve):
                n = 0

                def link(ins):
                    nonlocal n
                    n += 1
                    ins.then_inc(s_d5, 1)
                    dve.wait_ge(s_d5, n)

                for b, ts in enumerate(tiles):
                    dve.wait_ge(s_back, b + 1)
                    a = xn[:, ts[0]:ts[-1] + 1, :]
                    dve.tensor_tensor(a, a, ps[:, b % 4, 0:len(ts) * D].rearrange("p (t c) -> p t c", c=D), ALU.add).then_inc(s_res, 1)
                dve.wait_ge(s_res, NB)
                layer_norm(dve, link, s_ask5, s_root5, 1).then_inc(s_fin, 1)

            @block.sync
            def _(sp):
                sp.wait_ge(s_fin, 1)
                sp.dma_start(out[0:(NT - 1) * P, :].rearrange("(t p) c -> p t c", p=P), xn[:, 0:NT - 1, :]).then_inc(s_out, 16)
                sp.dma_start(out[(NT - 1) * P:N, :], xn[0:N - (NT - 1) * P, NT - 1, :]).then_inc(s_out, 16)
                sp.wait_ge(s_out, 32)


_RENAME = dict(
    Wn="L0_gnn_W_node", bn="L0_gnn_b_node", gn="L0_gnn_g_node", betan="L0_gnn_beta_node",
    We="L0_gnn_W_edge", be="L0_gnn_b_edge", ge="L0_gnn_g_edge", betae="L0_gnn_beta_edge",
    Wm="L0_gnn_W_msg", bm="L0_gnn_b_msg", gm="L0_gnn_g_msg", betam="L0_gnn_beta_msg",
    Wl="L1_gnn_W", att_src="L1_gnn_att_src", att_dst="L1_gnn_att_dst", bias="L1_gnn_bias")
_ORDER = ["x", "xT", "src", "dst", "edgeT", "Wn", "bn", "gn", "betan", "We", "be", "ge", "betae",
          "Wm", "bm", "gm", "betam", "Wl", "WlT", "att_src", "att_dst", "bias"]


def kernel(**inputs):
    import numpy as _np
    import concourse.bacc as _bacc
    from concourse import mybir as _mybir
    from concourse.bass_utils import run_bass_kernel_spmd as _run

    given = {k: _np.ascontiguousarray(inputs[v]) for k, v in _RENAME.items()}
    x = _np.ascontiguousarray(inputs["x"])
    given["x"] = x
    given["xT"] = _np.concatenate([x.T, _np.zeros((D, NPAD - N), x.dtype)], axis=1)
    source, target = _np.asarray(inputs["src"]), _np.asarray(inputs["dst"])
    given["src"] = _np.concatenate([source, _np.zeros(EPAD - E, source.dtype)])
    given["dst"] = _np.concatenate([target, _np.full(EPAD - E, NPAD - 1, target.dtype)])
    attr = _np.asarray(inputs["edge_attr_4"])
    given["edgeT"] = _np.concatenate([attr.T, _np.zeros((DE, EPAD - E), attr.dtype)], axis=1)
    given["WlT"] = _np.ascontiguousarray(_np.transpose(given["Wl"], (0, 2, 1)))

    nc = _bacc.Bacc("TRN2", target_bir_lowering=False, num_devices=1)
    arrays, args = {}, []
    for name in _ORDER:
        a = _np.ascontiguousarray(given[name])
        arrays[f"in_{name}_dram"] = a
        args.append(nc.dram_tensor(f"in_{name}_dram", a.shape, _mybir.dt.from_np(a.dtype), kind="ExternalInput").ap())
    args.append(nc.dram_tensor("out_0_dram", (N, D), _mybir.dt.float32, kind="ExternalOutput").ap())
    gnn_kernel(nc, *args)
    r = _run(nc, [arrays], core_ids=[0])
    return r.results[0]["out_0_dram"]
```
